# Optimizing a Trainium2 kernel written in Bass

```python
import numpy as np
import jax
import jax.numpy as jnp

def _softmax(x, axis=-1):
    return jax.nn.softmax(x, axis=axis)

def _gelu(x):
    return jax.nn.gelu(x, approximate=True)

def _silu(x):
    return jax.nn.silu(x)

def _sigmoid(x):
    return jax.nn.sigmoid(x)

def _layernorm(x, axis=-1, eps=1e-05):
    m = jnp.mean(x, axis=axis, keepdims=True)
    v = jnp.var(x, axis=axis, keepdims=True)
    return (x - m) / jnp.sqrt(v + eps)

def _scatter_add(tgt, idx, src, axis=0):
    return tgt.at[idx].add(src)

def _segment_sum(src, seg, n):
    return jax.ops.segment_sum(src, seg, n)
kernel_name = 'mk_lm_tower_d2_tok_ids256_r4_7c9a2e'

def setup_inputs(seed: int=0):
    np.random.seed(seed)
    _w = jnp.asarray

    def _rec_inputs():
        import jax
        import jax.numpy as jnp
        _rk = jax.random.key(seed)
        x = jax.random.randint(jax.random.fold_in(_rk, 1), (64, 256), 0, 256, jnp.int32)
        return x
    x = _rec_inputs()

    def _L0_tok_setup():
        import jax, jax.numpy as jnp
        import numpy as np
        VOCAB, D_MODEL, EMBED = (256, 64, 64)
        EPS = 1e-05

        def _layernorm(x, gamma, beta):
            mu = jnp.mean(x, axis=-1, keepdims=True)
            var = jnp.mean(jnp.square(x - mu), axis=-1, keepdims=True)
            return (x - mu) * jax.lax.rsqrt(var + EPS) * gamma + beta
        key = jax.random.key(seed)
        ks = jax.random.split(key, 8)
        tokens = jax.random.randint(ks[0], (64, 512), 0, VOCAB, dtype=jnp.int64 if jax.config.jax_enable_x64 else jnp.int32)
        emb_table = jax.random.normal(ks[1], (VOCAB, EMBED), dtype=jnp.float32)
        emb_table = emb_table.at[0].set(0.0)
        s1 = 1.0 / np.sqrt(EMBED + D_MODEL)
        W1 = jax.random.uniform(ks[2], (D_MODEL, EMBED + D_MODEL), minval=-s1, maxval=s1, dtype=jnp.float32)
        b1 = jax.random.uniform(ks[3], (D_MODEL,), minval=-s1, maxval=s1, dtype=jnp.float32)
        s2 = 1.0 / np.sqrt(D_MODEL)
        W2 = jax.random.uniform(ks[4], (D_MODEL, D_MODEL), minval=-s2, maxval=s2, dtype=jnp.float32)
        b2 = jax.random.uniform(ks[5], (D_MODEL,), minval=-s2, maxval=s2, dtype=jnp.float32)
        gamma = jnp.ones((D_MODEL,), dtype=jnp.float32)
        beta = jnp.zeros((D_MODEL,), dtype=jnp.float32)
        return {'tokens': tokens, 'emb_table': emb_table, 'W1': W1, 'b1': b1, 'W2': W2, 'b2': b2, 'gamma': gamma, 'beta': beta}
    _L0_tok_all = _L0_tok_setup()
    _L0_tok_in = {k: v for k, v in _L0_tok_all.items() if k in ('emb_table', 'W1', 'b1', 'W2', 'b2', 'gamma', 'beta')}
    del _L0_tok_all

    def _L0_attn_setup():
        import jax, jax.numpy as jnp
        import numpy as np
        B, T, D = (4, 512, 64)
        W_LORA, A_LORA, G_LORA = (64, 64, 128)
        DECAY_SCALE = -0.6065306597126334
        EPS = D * 1e-05

        def _forward(x, x_mix, W_r, W_k, W_v, W_o, A_w, B_w, b_w, A_a, B_a, b_a, A_g, B_g, k_k, k_a, r_k, gn_w, gn_b):
            b, t, d = x.shape
            shifted = jnp.pad(x, ((0, 0), (1, 0), (0, 0)))[:, :-1]
            delta = shifted - x
            xr, xw, xk, xv, xa, xg = [x + delta * x_mix[i] for i in range(6)]
            r = xr @ W_r
            w = DECAY_SCALE * jax.nn.sigmoid(jnp.tanh(xw @ A_w) @ B_w + b_w)
            k = xk @ W_k
            v = xv @ W_v
            a = jax.nn.sigmoid(xa @ A_a @ B_a + b_a)
            g = jax.nn.sigmoid(xg @ A_g) @ B_g
            kk = k * k_k
            kk = kk / jnp.maximum(jnp.linalg.norm(kk, axis=-1, keepdims=True), 1e-12)
            k = k * (1.0 + (a - 1.0) * k_a)
            decay = jnp.exp(w)

            def step(S, inp):
                r_t, dec_t, k_t, v_t, kk_t, a_t = inp
                b_t = kk_t * a_t
                sa = jnp.einsum('bvk,bk->bv', S, -kk_t)
                S = S * dec_t[:, None, :] + sa[:, :, None] * b_t[:, None, :] + v_t[:, :, None] * k_t[:, None, :]
                o_t = jnp.einsum('bvk,bk->bv', S, r_t)
                return (S, o_t)
            tm = lambda z: jnp.swapaxes(z, 0, 1)
            S0 = jnp.zeros((b, d, d), x.dtype)
            _, o = jax.lax.scan(step, S0, (tm(r), tm(decay), tm(k), tm(v), tm(kk), tm(a)))
            o = jnp.swapaxes(o, 0, 1)
            mu = jnp.mean(o, axis=-1, keepdims=True)
            var = jnp.var(o, axis=-1, keepdims=True)
            o = (o - mu) * jax.lax.rsqrt(var + EPS) * gn_w + gn_b
            o = o + jnp.sum(r * k * r_k, axis=-1, keepdims=True) * v
            return o * g @ W_o
        key = jax.random.key(seed)
        ks = jax.random.split(key, 20)
        n = jax.random.normal
        p = {}
        p['x'] = n(ks[0], (B, T, D), jnp.float32)
        p['x_mix'] = n(ks[1], (6, D), jnp.float32) * 0.1
        s = 1.0 / np.sqrt(D).astype(np.float32)
        p['W_r'] = n(ks[2], (D, D), jnp.float32) * s
        p['W_k'] = n(ks[3], (D, D), jnp.float32) * s
        p['W_v'] = n(ks[4], (D, D), jnp.float32) * s
        p['W_o'] = n(ks[5], (D, D), jnp.float32) * s
        p['A_w'] = n(ks[6], (D, W_LORA), jnp.float32) * s
        p['B_w'] = n(ks[7], (W_LORA, D), jnp.float32) / np.sqrt(W_LORA).astype(np.float32)
        p['b_w'] = n(ks[8], (D,), jnp.float32) * 0.5
        p['A_a'] = n(ks[9], (D, A_LORA), jnp.float32) * s
        p['B_a'] = n(ks[10], (A_LORA, D), jnp.float32) / np.sqrt(A_LORA).astype(np.float32)
        p['b_a'] = n(ks[11], (D,), jnp.float32) * 0.1
        p['A_g'] = n(ks[12], (D, G_LORA), jnp.float32) * s
        p['B_g'] = n(ks[13], (G_LORA, D), jnp.float32) / np.sqrt(G_LORA).astype(np.float32)
        p['k_k'] = n(ks[14], (D,), jnp.float32) * 0.5 + 0.85
        p['k_a'] = n(ks[15], (D,), jnp.float32) * 0.1 + 1.0
        p['r_k'] = n(ks[16], (D,), jnp.float32) * 0.1
        p['gn_w'] = jnp.ones((D,), jnp.float32)
        p['gn_b'] = jnp.zeros((D,), jnp.float32)
        return p
    _L0_attn_all = _L0_attn_setup()
    _L0_attn_in = {k: v for k, v in _L0_attn_all.items() if k in ('x_mix', 'W_r', 'W_k', 'W_v', 'W_o', 'A_w', 'B_w', 'b_w', 'A_a', 'B_a', 'b_a', 'A_g', 'B_g', 'k_k', 'k_a', 'r_k', 'gn_w', 'gn_b')}
    del _L0_attn_all

    def _L0_ffn_setup():
        import jax, jax.numpy as jnp
        import numpy as np
        E = 8
        K = 2
        D = 64
        H = 128
        DOUT = 64
        EPS = 1e-05
        key = jax.random.key(seed)
        ks = jax.random.split(key, 9)
        s = 0.02
        return {'x': jax.random.normal(ks[0], (4, 2048, D), jnp.float32), 'gamma': 1.0 + 0.05 * jax.random.normal(ks[1], (D,), jnp.float32), 'beta': 0.05 * jax.random.normal(ks[2], (D,), jnp.float32), 'Wr': 0.01 * jax.random.normal(ks[3], (D, E), jnp.float32), 'br': jnp.zeros((E,), jnp.float32), 'W1': s * jax.random.normal(ks[4], (E, D, H), jnp.float32), 'b1': s * jax.random.normal(ks[5], (E, H), jnp.float32), 'W2': s * jax.random.normal(ks[6], (E, H, DOUT), jnp.float32), 'b2': s * jax.random.normal(ks[7], (E, DOUT), jnp.float32)}
    _L0_ffn_all = _L0_ffn_setup()
    _L0_ffn_in = {k: v for k, v in _L0_ffn_all.items() if k in ('gamma', 'beta', 'Wr', 'br', 'W1', 'b1', 'W2', 'b2')}
    del _L0_ffn_all

    def _L1_attn_setup():
        import jax, jax.numpy as jnp
        import numpy as np
        B, N, C = (2, 12500, 64)
        H, W = (8, 64)
        HD = C // H
        key = jax.random.key(seed)
        k1, k2, k3, k4, k5 = jax.random.split(key, 5)
        s = 1.0 / np.sqrt(C)
        return {'x': jax.random.normal(k1, (B, N, C), dtype=jnp.float32), 'qkv_w': jax.random.uniform(k2, (C, 3 * C), jnp.float32, -s, s), 'qkv_b': jax.random.uniform(k3, (3 * C,), jnp.float32, -s, s), 'proj_w': jax.random.uniform(k4, (C, C), jnp.float32, -s, s), 'proj_b': jax.random.uniform(k5, (C,), jnp.float32, -s, s)}
    _L1_attn_all = _L1_attn_setup()
    _L1_attn_in = {k: v for k, v in _L1_attn_all.items() if k in ('qkv_w', 'qkv_b', 'proj_w', 'proj_b')}
    del _L1_attn_all

    def _L1_ffn_setup():
        import jax, jax.numpy as jnp
        import numpy as np
        B, N, D = (16, 1024, 64)
        NUM_EXPERTS, TOP_K, HEADS = (4, 2, 4)
        N_EDGES = 262144
        LN_EPS = 1e-05

        def _layernorm(x, g, b):
            mu = x.mean(-1, keepdims=True)
            var = ((x - mu) ** 2).mean(-1, keepdims=True)
            return (x - mu) * jax.lax.rsqrt(var + LN_EPS) * g + b

        def _forward(x, edge_index, W_gat, att_src, att_dst, b_gat, ln_gamma, ln_beta, W1, b1, W2, b2):
            Bc, Nc, Dc = x.shape
            M = Bc * Nc
            x_flat = x.reshape(M, Dc)
            h = (x_flat @ W_gat).reshape(M, HEADS, NUM_EXPERTS)
            loops = jnp.arange(M, dtype=edge_index.dtype)
            src = jnp.concatenate([edge_index[0], loops])
            dst = jnp.concatenate([edge_index[1], loops])
            a_src = (h * att_src).sum(-1)
            a_dst = (h * att_dst).sum(-1)
            e = jax.nn.leaky_relu(a_src[src] + a_dst[dst], negative_slope=0.2)
            e_max = jax.ops.segment_max(e, dst, num_segments=M)
            ee = jnp.exp(e - e_max[dst])
            denom = jax.ops.segment_sum(ee, dst, num_segments=M)
            alpha = ee / (denom[dst] + 1e-16)
            msg = h[src] * alpha[:, :, None]
            agg = jax.ops.segment_sum(msg, dst, num_segments=M).reshape(M, HEADS * NUM_EXPERTS) + b_gat
            scores = _layernorm(agg, ln_gamma, ln_beta).reshape(M, HEADS, NUM_EXPERTS).mean(1)
            scores = scores.reshape(Bc, Nc, NUM_EXPERTS)
            topk_s, topk_i = jax.lax.top_k(scores, TOP_K)
            w = jax.nn.softmax(topk_s, axis=-1)
            out = jnp.zeros_like(x)
            for ei in range(NUM_EXPERTS):
                g = jnp.where(topk_i == ei, w, 0.0).sum(-1)
                hh = jax.nn.gelu(x @ W1[ei] + b1[ei], approximate=False)
                out = out + g[..., None] * (hh @ W2[ei] + b2[ei])
            return out
        key = jax.random.key(seed)
        ks = jax.random.split(key, 8)
        s = 0.05
        return {'x': jax.random.normal(ks[0], (B, N, D), jnp.float32), 'W_gat': jax.random.normal(ks[1], (D, HEADS * NUM_EXPERTS), jnp.float32) * s, 'att_src': jax.random.normal(ks[2], (HEADS, NUM_EXPERTS), jnp.float32) * s, 'att_dst': jax.random.normal(ks[3], (HEADS, NUM_EXPERTS), jnp.float32) * s, 'b_gat': jnp.zeros((HEADS * NUM_EXPERTS,), jnp.float32), 'ln_gamma': jnp.ones((HEADS * NUM_EXPERTS,), jnp.float32), 'ln_beta': jnp.zeros((HEADS * NUM_EXPERTS,), jnp.float32), 'W1': jax.random.normal(ks[4], (NUM_EXPERTS, D, 2 * D), jnp.float32) * s, 'b1': jnp.zeros((NUM_EXPERTS, 2 * D), jnp.float32), 'W2': jax.random.normal(ks[5], (NUM_EXPERTS, 2 * D, D), jnp.float32) * s, 'b2': jnp.zeros((NUM_EXPERTS, D), jnp.float32), 'edge_index': jax.random.randint(ks[6], (2, N_EDGES), 0, B * N, jnp.int32)}
    _L1_ffn_all = _L1_ffn_setup()
    _L1_ffn_in = {k: v for k, v in _L1_ffn_all.items() if k in ('W_gat', 'att_src', 'att_dst', 'b_gat', 'ln_gamma', 'ln_beta', 'W1', 'b1', 'W2', 'b2', 'edge_index')}
    del _L1_ffn_all
    return {'x': x, 'L0_tok_emb_table': _L0_tok_in['emb_table'], 'L0_tok_W1': _L0_tok_in['W1'], 'L0_tok_b1': _L0_tok_in['b1'], 'L0_tok_W2': _L0_tok_in['W2'], 'L0_tok_b2': _L0_tok_in['b2'], 'L0_tok_gamma': _L0_tok_in['gamma'], 'L0_tok_beta': _L0_tok_in['beta'], 'L0_attn_x_mix': _L0_attn_in['x_mix'], 'L0_attn_W_r': _L0_attn_in['W_r'], 'L0_attn_W_k': _L0_attn_in['W_k'], 'L0_attn_W_v': _L0_attn_in['W_v'], 'L0_attn_W_o': _L0_attn_in['W_o'], 'L0_attn_A_w': _L0_attn_in['A_w'], 'L0_attn_B_w': _L0_attn_in['B_w'], 'L0_attn_b_w': _L0_attn_in['b_w'], 'L0_attn_A_a': _L0_attn_in['A_a'], 'L0_attn_B_a': _L0_attn_in['B_a'], 'L0_attn_b_a': _L0_attn_in['b_a'], 'L0_attn_A_g': _L0_attn_in['A_g'], 'L0_attn_B_g': _L0_attn_in['B_g'], 'L0_attn_k_k': _L0_attn_in['k_k'], 'L0_attn_k_a': _L0_attn_in['k_a'], 'L0_attn_r_k': _L0_attn_in['r_k'], 'L0_attn_gn_w': _L0_attn_in['gn_w'], 'L0_attn_gn_b': _L0_attn_in['gn_b'], 'L0_ffn_gamma': _L0_ffn_in['gamma'], 'L0_ffn_beta': _L0_ffn_in['beta'], 'L0_ffn_Wr': _L0_ffn_in['Wr'], 'L0_ffn_br': _L0_ffn_in['br'], 'L0_ffn_W1': _L0_ffn_in['W1'], 'L0_ffn_b1': _L0_ffn_in['b1'], 'L0_ffn_W2': _L0_ffn_in['W2'], 'L0_ffn_b2': _L0_ffn_in['b2'], 'L1_attn_qkv_w': _L1_attn_in['qkv_w'], 'L1_attn_qkv_b': _L1_attn_in['qkv_b'], 'L1_attn_proj_w': _L1_attn_in['proj_w'], 'L1_attn_proj_b': _L1_attn_in['proj_b'], 'L1_ffn_W_gat': _L1_ffn_in['W_gat'], 'L1_ffn_att_src': _L1_ffn_in['att_src'], 'L1_ffn_att_dst': _L1_ffn_in['att_dst'], 'L1_ffn_b_gat': _L1_ffn_in['b_gat'], 'L1_ffn_ln_gamma': _L1_ffn_in['ln_gamma'], 'L1_ffn_ln_beta': _L1_ffn_in['ln_beta'], 'L1_ffn_W1': _L1_ffn_in['W1'], 'L1_ffn_b1': _L1_ffn_in['b1'], 'L1_ffn_W2': _L1_ffn_in['W2'], 'L1_ffn_b2': _L1_ffn_in['b2'], 'L1_ffn_edge_index': _L1_ffn_in['edge_index']}

def reference(x, L0_tok_emb_table, L0_tok_W1, L0_tok_b1, L0_tok_W2, L0_tok_b2, L0_tok_gamma, L0_tok_beta, L0_attn_x_mix, L0_attn_W_r, L0_attn_W_k, L0_attn_W_v, L0_attn_W_o, L0_attn_A_w, L0_attn_B_w, L0_attn_b_w, L0_attn_A_a, L0_attn_B_a, L0_attn_b_a, L0_attn_A_g, L0_attn_B_g, L0_attn_k_k, L0_attn_k_a, L0_attn_r_k, L0_attn_gn_w, L0_attn_gn_b, L0_ffn_gamma, L0_ffn_beta, L0_ffn_Wr, L0_ffn_br, L0_ffn_W1, L0_ffn_b1, L0_ffn_W2, L0_ffn_b2, L1_attn_qkv_w, L1_attn_qkv_b, L1_attn_proj_w, L1_attn_proj_b, L1_ffn_W_gat, L1_ffn_att_src, L1_ffn_att_dst, L1_ffn_b_gat, L1_ffn_ln_gamma, L1_ffn_ln_beta, L1_ffn_W1, L1_ffn_b1, L1_ffn_W2, L1_ffn_b2, L1_ffn_edge_index):
    import jax
    import jax.numpy as jnp

    def _L0_tok_ref(tokens, emb_table, W1, b1, W2, b2, gamma, beta):
        import jax, jax.numpy as jnp
        import numpy as np
        VOCAB, D_MODEL, EMBED = (256, 64, 64)
        EPS = 1e-05

        def _layernorm(x, gamma, beta):
            mu = jnp.mean(x, axis=-1, keepdims=True)
            var = jnp.mean(jnp.square(x - mu), axis=-1, keepdims=True)
            return (x - mu) * jax.lax.rsqrt(var + EPS) * gamma + beta
        emb = emb_table[tokens]
        W1_emb = W1[:, :EMBED]
        h = jax.nn.relu(jnp.einsum('bue,de->bud', emb, W1_emb) + b1)
        out = jnp.einsum('bud,od->buo', h, W2) + b2
        return _layernorm(out, gamma, beta)

    def _L0_attn_ref(x, x_mix, W_r, W_k, W_v, W_o, A_w, B_w, b_w, A_a, B_a, b_a, A_g, B_g, k_k, k_a, r_k, gn_w, gn_b):
        import jax, jax.numpy as jnp
        import numpy as np
        B, T, D = (4, 512, 64)
        W_LORA, A_LORA, G_LORA = (64, 64, 128)
        DECAY_SCALE = -0.6065306597126334
        EPS = D * 1e-05

        def _forward(x, x_mix, W_r, W_k, W_v, W_o, A_w, B_w, b_w, A_a, B_a, b_a, A_g, B_g, k_k, k_a, r_k, gn_w, gn_b):
            b, t, d = x.shape
            shifted = jnp.pad(x, ((0, 0), (1, 0), (0, 0)))[:, :-1]
            delta = shifted - x
            xr, xw, xk, xv, xa, xg = [x + delta * x_mix[i] for i in range(6)]
            r = xr @ W_r
            w = DECAY_SCALE * jax.nn.sigmoid(jnp.tanh(xw @ A_w) @ B_w + b_w)
            k = xk @ W_k
            v = xv @ W_v
            a = jax.nn.sigmoid(xa @ A_a @ B_a + b_a)
            g = jax.nn.sigmoid(xg @ A_g) @ B_g
            kk = k * k_k
            kk = kk / jnp.maximum(jnp.linalg.norm(kk, axis=-1, keepdims=True), 1e-12)
            k = k * (1.0 + (a - 1.0) * k_a)
            decay = jnp.exp(w)

            def step(S, inp):
                r_t, dec_t, k_t, v_t, kk_t, a_t = inp
                b_t = kk_t * a_t
                sa = jnp.einsum('bvk,bk->bv', S, -kk_t)
                S = S * dec_t[:, None, :] + sa[:, :, None] * b_t[:, None, :] + v_t[:, :, None] * k_t[:, None, :]
                o_t = jnp.einsum('bvk,bk->bv', S, r_t)
                return (S, o_t)
            tm = lambda z: jnp.swapaxes(z, 0, 1)
            S0 = jnp.zeros((b, d, d), x.dtype)
            _, o = jax.lax.scan(step, S0, (tm(r), tm(decay), tm(k), tm(v), tm(kk), tm(a)))
            o = jnp.swapaxes(o, 0, 1)
            mu = jnp.mean(o, axis=-1, keepdims=True)
            var = jnp.var(o, axis=-1, keepdims=True)
            o = (o - mu) * jax.lax.rsqrt(var + EPS) * gn_w + gn_b
            o = o + jnp.sum(r * k * r_k, axis=-1, keepdims=True) * v
            return o * g @ W_o
        return _forward(x, x_mix, W_r, W_k, W_v, W_o, A_w, B_w, b_w, A_a, B_a, b_a, A_g, B_g, k_k, k_a, r_k, gn_w, gn_b)

    def _L0_ffn_ref(x, gamma, beta, Wr, br, W1, b1, W2, b2):
        import jax, jax.numpy as jnp
        import numpy as np
        E = 8
        K = 2
        D = 64
        H = 128
        DOUT = 64
        EPS = 1e-05
        mu = jnp.mean(x, axis=-1, keepdims=True)
        var = jnp.mean(jnp.square(x - mu), axis=-1, keepdims=True)
        xn = (x - mu) * jax.lax.rsqrt(var + EPS) * gamma + beta
        logits = jnp.einsum('bsd,de->bse', xn, Wr) + br
        top_vals, top_idx = jax.lax.top_k(logits, K)
        w = jax.nn.softmax(top_vals, axis=-1)
        w_full = jnp.einsum('bsk,bske->bse', w, jax.nn.one_hot(top_idx, E, dtype=w.dtype))
        y = jnp.zeros(x.shape[:-1] + (DOUT,), x.dtype)
        for e in range(E):
            h = jax.nn.gelu(jnp.einsum('bsd,dh->bsh', xn, W1[e]) + b1[e], approximate=False)
            y_e = jnp.einsum('bsh,hd->bsd', h, W2[e]) + b2[e]
            y = y + y_e * w_full[..., e, None]
        return y

    def _L1_attn_ref(x, qkv_w, qkv_b, proj_w, proj_b):
        import jax, jax.numpy as jnp
        import numpy as np
        B, N, C = (2, 12500, 64)
        H, W = (8, 64)
        HD = C // H
        Bv, Nv, Cv = x.shape
        pad = (W - Nv % W) % W
        xp = jnp.pad(x, ((0, 0), (0, pad), (0, 0)))
        nW = (Nv + pad) // W
        xw = xp.reshape(Bv, nW, W, Cv)
        qkv = xw @ qkv_w + qkv_b
        qkv = qkv.reshape(Bv, nW, W, 3, H, HD)
        q, k, v = (qkv[..., 0, :, :], qkv[..., 1, :, :], qkv[..., 2, :, :])
        scale = HD ** (-0.5)
        attn = jnp.einsum('bwihd,bwjhd->bwhij', q, k) * scale
        attn = jax.nn.softmax(attn, axis=-1)
        out = jnp.einsum('bwhij,bwjhd->bwihd', attn, v)
        out = out.reshape(Bv, nW, W, Cv)
        out = out @ proj_w + proj_b
        out = out.reshape(Bv, nW * W, Cv)[:, :Nv]
        return out

    def _L1_ffn_ref(x, W_gat, att_src, att_dst, b_gat, ln_gamma, ln_beta, W1, b1, W2, b2, edge_index):
        import jax, jax.numpy as jnp
        import numpy as np
        B, N, D = (16, 1024, 64)
        NUM_EXPERTS, TOP_K, HEADS = (4, 2, 4)
        N_EDGES = 262144
        LN_EPS = 1e-05

        def _layernorm(x, g, b):
            mu = x.mean(-1, keepdims=True)
            var = ((x - mu) ** 2).mean(-1, keepdims=True)
            return (x - mu) * jax.lax.rsqrt(var + LN_EPS) * g + b

        def _forward(x, edge_index, W_gat, att_src, att_dst, b_gat, ln_gamma, ln_beta, W1, b1, W2, b2):
            Bc, Nc, Dc = x.shape
            M = Bc * Nc
            x_flat = x.reshape(M, Dc)
            h = (x_flat @ W_gat).reshape(M, HEADS, NUM_EXPERTS)
            loops = jnp.arange(M, dtype=edge_index.dtype)
            src = jnp.concatenate([edge_index[0], loops])
            dst = jnp.concatenate([edge_index[1], loops])
            a_src = (h * att_src).sum(-1)
            a_dst = (h * att_dst).sum(-1)
            e = jax.nn.leaky_relu(a_src[src] + a_dst[dst], negative_slope=0.2)
            e_max = jax.ops.segment_max(e, dst, num_segments=M)
            ee = jnp.exp(e - e_max[dst])
            denom = jax.ops.segment_sum(ee, dst, num_segments=M)
            alpha = ee / (denom[dst] + 1e-16)
            msg = h[src] * alpha[:, :, None]
            agg = jax.ops.segment_sum(msg, dst, num_segments=M).reshape(M, HEADS * NUM_EXPERTS) + b_gat
            scores = _layernorm(agg, ln_gamma, ln_beta).reshape(M, HEADS, NUM_EXPERTS).mean(1)
            scores = scores.reshape(Bc, Nc, NUM_EXPERTS)
            topk_s, topk_i = jax.lax.top_k(scores, TOP_K)
            w = jax.nn.softmax(topk_s, axis=-1)
            out = jnp.zeros_like(x)
            for ei in range(NUM_EXPERTS):
                g = jnp.where(topk_i == ei, w, 0.0).sum(-1)
                hh = jax.nn.gelu(x @ W1[ei] + b1[ei], approximate=False)
                out = out + g[..., None] * (hh @ W2[ei] + b2[ei])
            return out
        return _forward(x, edge_index, W_gat, att_src, att_dst, b_gat, ln_gamma, ln_beta, W1, b1, W2, b2)
    h = _L0_tok_ref(x, L0_tok_emb_table, L0_tok_W1, L0_tok_b1, L0_tok_W2, L0_tok_b2, L0_tok_gamma, L0_tok_beta)
    h = h + _L0_attn_ref(_layernorm(h, axis=-1), L0_attn_x_mix, L0_attn_W_r, L0_attn_W_k, L0_attn_W_v, L0_attn_W_o, L0_attn_A_w, L0_attn_B_w, L0_attn_b_w, L0_attn_A_a, L0_attn_B_a, L0_attn_b_a, L0_attn_A_g, L0_attn_B_g, L0_attn_k_k, L0_attn_k_a, L0_attn_r_k, L0_attn_gn_w, L0_attn_gn_b)
    h = h + _L0_ffn_ref(_layernorm(h, axis=-1), L0_ffn_gamma, L0_ffn_beta, L0_ffn_Wr, L0_ffn_br, L0_ffn_W1, L0_ffn_b1, L0_ffn_W2, L0_ffn_b2)
    h = h + _L1_attn_ref(_layernorm(h, axis=-1), L1_attn_qkv_w, L1_attn_qkv_b, L1_attn_proj_w, L1_attn_proj_b)
    h = h + _L1_ffn_ref(_layernorm(h, axis=-1), L1_ffn_W_gat, L1_ffn_att_src, L1_ffn_att_dst, L1_ffn_b_gat, L1_ffn_ln_gamma, L1_ffn_ln_beta, L1_ffn_W1, L1_ffn_b1, L1_ffn_W2, L1_ffn_b2, L1_ffn_edge_index)
    return h

_drawn_inputs = setup_inputs


def setup_inputs(seed=0):
    import zlib

    import numpy as np

    out = dict(_drawn_inputs(seed))
    spreads = {'L0_tok_gamma': (1.0, 0.2),
     'L0_tok_beta': (0.0, 0.1),
     'L0_attn_gn_w': (1.0, 0.2),
     'L0_attn_gn_b': (0.0, 0.1),
     'L0_ffn_br': (0.0, 0.522),
     'L1_ffn_b_gat': (0.0, 0.8),
     'L1_ffn_ln_gamma': (1.0, 0.6),
     'L1_ffn_ln_beta': (0.0, 2.0),
     'L1_ffn_b1': (0.0, 1.255),
     'L1_ffn_b2': (0.0, 0.463)}
    factors = {'L0_attn_b_a': 3.517,
     'L0_ffn_gamma': 8.0,
     'L0_ffn_beta': 8.0,
     'L0_ffn_Wr': 8.0,
     'L0_ffn_W1': 5.146,
     'L0_ffn_b1': 8.0,
     'L0_ffn_W2': 4.99,
     'L0_ffn_b2': 15.874,
     'L1_ffn_att_src': 64.0,
     'L1_ffn_att_dst': 64.0,
     'L1_attn_qkv_b': 6.514,
     'L1_attn_proj_b': 4.018,
     'L1_ffn_W_gat': 5.488}
    for name, (base, spread) in spreads.items():
        noise = np.random.default_rng([zlib.crc32(name.encode()), seed]).standard_normal(out[name].shape)
        drawn = base * np.exp(spread * noise) if base else spread * noise
        out[name] = jnp.asarray(drawn.astype(out[name].dtype))
    for name, factor in factors.items():
        out[name] = (out[name] * factor).astype(out[name].dtype)
    return out
```

```python
from contextlib import ExitStack
import numpy as np
import concourse.bass as bass
from concourse import mybir
ALU=mybir.AluOpType; ACT=mybir.ActivationFunctionType; AX=mybir.AxisListType
F32=mybir.dt.float32; I32=mybir.dt.int32; U32=mybir.dt.uint32; BF16=mybir.dt.bfloat16
P=128; D=64; M=16384; NT=M//P; EPS=1e-5
HALVES=[(0,slice(0,D)),(1,slice(D,P))]
GI=16
AI=32
T=256; C=64; NC=T//C; LANES=2; ITERS=64//2//LANES
DECAY=-0.6065306597126334
PE_STEPS="xg h0 proj glin vtok zz ss BKt At gtk bon G1 G2 L p2 x2 p4 x4 p8 x8 EE MKV E2 Z0 Z1 W W1T Sp0 O0 U1 Sp1 O1 U2 Sp2 O2 U3 O3 yT wo".split()
ACT_STEPS="h0s xs V th za sgt tw ta sq e1 e2 e3 lnk rn BKs Ats gts bons p2s p4s p8s EEs MKVs E2s Z0s W1Ts S1 S2 S3 Os osq lnv rstd yTs".split()
DVE_STEPS="oneh sg w cs cm a kq ssm kn A R b0 B t1 kp K rk g1 g2 l o d1 d2 d4 d8 Z1 W U1 U2 U3 mu oc var on gw gb bv ob og h".split()
COLS="b_w b_a k_k k_a r_k mr mw mk mv ma mg b_w2 b_a2 nk_a".split()
F_STEPS=dict(
    pe=["xT","lg","h0","h1"]+[s for e in range(8) for s in ([f"y{e}",f"h{e+2}"] if e<6 else [f"y{e}"])]+["wT","bias"],
    act=["xTs","lgs","th"]+[f"g{e}" for e in range(8)]+["wTs"],
    dve="xg xb mx mi mf dd w1 w2 q0 q1 q0w q1w wf".split()+[f"{s}{p}" for p in range(4) for s in ("ym","ya","yb")]+["ab","h"])
A_STEPS=dict(pe="xT qkv sc PT pv oT pj".split(), act="xs xTs q ex PTs oTs".split(), dve="kb vb mx sb sm rc on h".split())
G_STEPS=dict(pe="xT hg".split(), act="xs xTs hgs".split(), dve="ms rs md rd".split())
Y_STEPS=dict(pe=["h0","h1","y0","h2","y1","h3","y2","y3"], act=[f"g{e}" for e in range(4)], dve=["b0","b1"])
NE=262144; EC=NE//P
EW=2304
SW=EW+NT
KS=32768
SENT=float(NT*KS)
OOB=float(1<<20)
BIG=1e30
ROW=24
CH=152; NCH=SW//CH
assert CH*NCH==SW

class Lane:
    def __init__(self,banks,pe,act,dve,first):
        self.ps=banks; self.pe=pe; self.act=act; self.dve=dve; self.first=first

def sort_steps(n):
    steps=[]; k=2
    while True:
        flip=[]; nb,rem=n//k,n%k
        if nb: flip.append(("flip",0,nb,k))
        if rem:
            s=nb*k
            if rem>k//2:
                c=rem-k//2
                flip.append(("rflip",s,k//2,c)); flip.append(("copy",s,0,k//2-c))
            else: flip.append(("copy",s,0,rem))
        steps.append(flip)
        d=k//4
        while d>=1:
            st=[]; b=2*d; nb,rem=n//b,n%b
            if nb: st.append(("half",0,nb,b))
            if rem:
                s=nb*b
                if rem>d:
                    c=rem-d
                    st.append(("rhalf",s,d,c)); st.append(("copy",s+c,0,d-c)) if d>c else None
                else: st.append(("copy",s,0,rem))
            steps.append(st); d//=2
        if k>=n: break
        k*=2
    return steps

SORT_ITERS=5
O_STEPS=16
GN=SW//32; GPY=GN//(GI-1)

def prog(nc, x, embT_d, w1T_d, tb1_d, w2T_d, rows_d, proj_d, wv_d, ag_d, lora_d, bg_d, wo_d, cols_d,
         gam_d, wr_d, w1_d, b1_d, w2_d, b2_d, qkv_d, proj1_d, wg_d, att_d, lw1_d, lb1_d, lw2_d, lb2_d, fin_d, edges, out):
    with ExitStack() as ctx:
        sb=lambda n,s,d=F32: ctx.enter_context(nc.sbuf_tensor(n,s,d))
        pt=lambda n,s,d=F32: ctx.enter_context(nc.psum_tensor(n,s,d))
        sem=lambda n: ctx.enter_context(nc.semaphore(n))
        dram=lambda n,s,d=F32: nc.dram_tensor(n,s,d,kind="Internal").ap()
        xTd=dram("xT_d",(32*D,512)); tbl=dram("node_table",(M,ROW)); yd=dram("expert_out",(M,4*D))
        buck=dram("buck",(P*EW,1)); rows_e=dram("rows_sorted",(P*SW,ROW)); sums_d=dram("sums_sorted",(P*SW,ROW))
        rank_d=dram("edge_ranks",(P,EC)); state_d=dram("node_state",(M,ROW))
        H=sb("h_res",[P,NT,D]); ident=sb("ident",[P,P]); ones_f=sb("ones_f",[P,P])
        A0=0; B0=2*SW; C0=B0+3*SW+4; D0=C0+8*SW; TOTAL=42700; SC0=TOTAL-2*EC
        arena=sb("arena",[P,TOTAL])
        def bump(off,end):
            at=[off]
            def take(shape,dt=F32):
                n=int(np.prod(shape)); n=n if dt!=BF16 else (n+1)//2
                v=arena[:,at[0]:at[0]+n]; at[0]+=n
                assert at[0]<=end,(at[0],end)
                if dt!=F32: v=v.bitcast(dt)
                if len(shape)==2: v=v.rearrange("p (a b) -> p a b",b=shape[1])
                if len(shape)==3: v=v.rearrange("p (a b c) -> p a b c",b=shape[1],c=shape[2])
                return v
            take.at=at
            return take
        PS=[pt(f"bank{k}",[P,512]) for k in range(8)]
        iota_i=sb("iota_i",[P,P],I32); iota_b=sb("iota_b",[P,P],BF16)
        tri=sb("tri",[P,P],BF16); anti=sb("anti",[P,P],BF16); ones_b=sb("ones_b",[P,P],BF16); zero_b=sb("zero_b",[P,P],BF16)
        idx16=sb("idx16",[P,2,16],I32); key16=sb("key16",[P,2,16]); dumi=sb("dumi",[1,4])
        rowp_f=sb("rowp_f",[P,1]); rowp_i=sb("rowp_i",[P,1],I32); rowbase=sb("rowbase",[P,1]); nreal=sb("nreal",[P,1])
        gs=sb("gs",[P,2,16,ROW]); gidx16=sb("gidx16",[P,2,16],I32); carry=sb("carry",[P,2,ROW])
        scat=bump(SC0,TOTAL); idx_all=scat([EC],I32); key_all=scat([EC])
        sorting=bump(TOTAL-2*SW,TOTAL); K=[sorting([SW]),sorting([SW])]
        late=bump(A0,B0); heads=late([SW]); v8=late([P]); endf=late([P]); end_i=late([P],I32)
        late=bump(B0,C0); gidx=late([SW],I32); cont=late([SW]); neg=late([SW+1])
        terms=bump(C0,D0); asx=terms([4,SW]); adx=terms([4,SW])
        col_i=bump(C0,D0)([SW],I32)
        late=bump(D0,TOTAL); rch=late([2*CH,ROW]).rearrange("p (s c) f -> p s c f",s=2)
        endd=late([P,4])
        ends=bump(D0,TOTAL)([P,ROW])
        s_pair=sem("index_parts_ready"); s_gate=sem("pool_gate"); s_bn=sem("bounds_ready")
        s_ld=sem("edges_loaded"); s_const=sem("constants_ready"); s_v=sem("dve_step"); s_oh=sem("onehot_ready")
        s_pre=sem("prefix_ready"); s_post=sem("prefix_advanced"); s_rd=sem("rank_read"); s_stage=sem("ranks_staged")
        s_scat=[sem("scattered_0"),sem("scattered_1")]; s_fill=sem("buckets_filled"); s_sent=sem("sentinels_ready"); s_bk=sem("buckets_loaded")
        s_gat=[sem("gathered_0"),sem("gathered_1")]; s_acp=sem("attention_terms_copied"); s_rk=sem("ranks_ready"); s_rks=sem("ranks_stored")
        s_row=[sem("rows_stored_0"),sem("rows_stored_1")]; s_gi=sem("gather_indices_ready"); s_adm=sem("scores_ready"); s_exp=sem("exp_ready")
        s_rld=[sem("rows_loaded_0"),sem("rows_loaded_1")]; s_sum=sem("sums_ready"); s_sst=[sem("sums_stored_0"),sem("sums_stored_1")]
        s_ei=sem("end_indices_ready"); s_eg=sem("ends_gathered")
        front=bump(A0,TOTAL-2*SW)
        raw=front([4,P]); wx=front([4,P]); ws=front([4,P])
        vraw=front([D]); vx=front([D]); vs=front([D])
        graw=front([2,P]); gx=front([2,P]); gsf=front([2,P])
        lora=front([2,P]); bg=front([D]); wo=front([2,D])
        cols=front([len(COLS)]); rows=front([5,D])
        onesblk=front([P])
        tab=front([2,2*D]); tm=front([2,D]); tst=front([4])
        embT=front([256])[0:D]; w1T=front([D])[0:D]; w2T=front([D])[0:D]; tb1=front([1])[0:D]; hT=front([256])[0:D]
        mg1=front([2,D]); mg2=front([2,D]); ml=front([2,D]); i64=front([D])
        blk=front([D])[0:D]; mrep=front([6,D])[0:D]
        flag=front([T]); ip_i=front([2],I32); ip=front([2])
        jb_i=front([D],I32)[0:D]; pb_i=front([1],I32)[0:D]; pb_f=front([1])[0:D]; lnb=front([2])
        s_tv=sem("table_variance")
        early=bump(front.at[0],SC0)
        dst_i=early([EC],I32); src_i=early([EC],I32); tmp_i=early([EC],I32); bkt_f=early([EC]); rank_f=early([EC])
        bkt_b=early([EC+32],BF16); oh=early([2*4,P],BF16).rearrange("p (s u) e -> p s u e",s=2); junk=early([4,P],BF16)
        rank16=early([2,16]); ovf16=early([2,16]); idxf16=early([2,16]); sent=early([EW])
        L=[]
        for l in range(LANES):
            B=Lane(PS[4*l:4*l+4],sem(f"pe_step_{l}"),sem(f"act_step_{l}"),sem(f"dve_step_{l}"),1); L.append(B)
            B.ld=sem(f"tokens_loaded_{l}"); B.tk=front([512],I32)
            B.oneh=front([2,512]); B.x=front([257]); B.h0=front([4,D]); B.th=front([T]); B.za=front([T])
            B.sg=front([2,T]); B.w=front([T]); B.a=front([T]); B.cs=front([T]); B.e1=front([T])
            B.e2=front([T]); B.e3=front([T]); B.kq=front([T]); B.kp=front([T])
            B.rk=front([T]); B.b0=front([T]); B.AR=front([4,2,D]); B.B=front([T]); B.K=front([T]); B.V=front([4,D])
            B.gt=front([4,D]); B.bon=front([4]); B.BK=front([2,4,D]); B.YA=front([4,2,D]); B.g1=front([4,2,D])
            B.g2=front([4,2,D]); B.lo=front([2,4,D]); B.pp=front([2,4,D]); B.p4=front([2,4,D]); B.p8=front([4,D])
            B.dta=front([4,D]); B.dtb=front([4,D]); B.EE=front([2,4,D]); B.E2=front([4,D]); B.Z0=front([4,2,D])
            B.Z1=front([4,2,D]); B.Wy=front([4,2,D]); B.W1T=front([4,D]); B.U=front([4,D]); B.S=front([4,D])
            B.O=front([4,D]); B.oc=front([4,D]); B.osq=front([4,D]); B.st=front([4,4]); B.yT=front([T])
            B.sq=B.osq.rearrange("p c d -> p (c d)"); B.rn=B.yT; B.cm=B.O.rearrange("p c d -> p (c d)")
        s_w=sem("weights_loaded"); s_c=sem("masks_ready"); s_cb=sem("masks_copied"); s_prep=sem("weights_ready"); 
        s_t=sem("table_matmul"); s_ta=sem("table_act"); s_tt=sem("table_ready"); s_out=sem("out_stored"); s_z=sem("zeros_ready"); s_g=sem("pool_chain")
        col=lambda n: cols[:,COLS.index(n):COLS.index(n)+1]
        STEPS=dict(pe=PE_STEPS,act=ACT_STEPS,dve=DVE_STEPS)
        def mk(eng,me):
            def wait(l,i,*names):
                for e,st,sm in (("pe",PE_STEPS,L[l].pe),("act",ACT_STEPS,L[l].act),("dve",DVE_STEPS,L[l].dve)):
                    at=[st.index(nm.split(":")[1]) for nm in names if nm.split(":")[0]==e]
                    if at: eng.wait_ge(sm,i*len(st)+max(at)+(2 if e=="dve" else 1))
                if me=="pe": nc.tensor.ldweights(zero_b[:,:],tile_position=(0,0))
            return wait
        def c4(t): return t.rearrange("p (c t) -> p c t",c=4)
        halves=HALVES

        s_mc=sem("layer_masks_ready")
        con=bump(D0+4400,TOTAL-2*SW)
        fgam=con([2,D]); fwr=con([8]); fw1=con([8,P]); fb1=con([8]); fw2=con([8,D]); fb2=con([D])
        con2=bump(D0+5130,SC0)
        aw=con2([3*D]); ap=con2([D]); hmask=con2([8]); vmask=con2([2])
        gw=con2([16]); gatt=con2([2,16]); lw1=con2([4,P]); lb1=con2([4]); lw2=con2([4,D]); lb2=con2([4,D])
        iot=sb("iota8",[P,8]); iot_i=sb("iota8_i",[P,8],I32); mk_i=sb("mask_iota",[P,2],I32); mkf=sb("mask_iota_f",[P,2])
        eps=sb("eps",[P,1])
        xn=bump(C0,D0)([NT,D])
        sq=bump(C0+8192,D0)([NT,D])
        lst=sb("ln_stat",[P,4,NT])
        s_la=sem("norm_to_act"); s_lb=sem("norm_from_act"); s_lc=sem("norm_log")
        def lanes(pref,n,banks,first=0):
            return [Lane(PS[l*banks:(l+1)*banks],sem(f"{pref}_pe_{l}"),sem(f"{pref}_act_{l}"),sem(f"{pref}_dve_{l}"),first) for l in range(n)]
        FL=lanes("ffn0",2,4); take=bump(C0+8192,D0)
        for B in FL:
            B.xs=take([4,D]); B.xT=take([512]); B.hT=take([2,512]); B.lg=take([4,8]); B.mx=take([4,8])
            B.mi=take([4,8],U32); B.mf=take([4,2]); B.dm=take([1]); B.dd=take([4]); B.w12=take([4,2])
            B.q=take([2,32]); B.wf=take([4,8]); B.tmp=take([4,2,D]); B.acc=take([4,D]); B.wTs=take([512])
        AL=lanes("attn1",4,2,first=1); take=bump(C0+8192,D0)
        for B in AL:
            B.xs=take([D]); B.xT=take([P]); B.Q=take([P]); B.K=take([8,D]); B.V=take([2,D]); B.E=take([8,D])
            B.PT=take([4,P]); B.mx=take([8]); B.rs=take([8]); B.o=take([D]); B.oT=take([P])
        GL=lanes("gat",2,4); take=bump(C0+8192,D0)
        for B in GL:
            B.xs=take([4,D]); B.xT=take([512]); B.row=take([4,24]); B.tm=take([4,16])
        YL=lanes("ffn1",2,4); take=bump(D0,D0+5130)
        for B in YL:
            B.xT=take([512]); B.hT=take([2,512]); B.ys=take([2,512])
        s_xst=[sem("xT_stored_0"),sem("xT_stored_1")]; s_tst=[sem("table_stored_0"),sem("table_stored_1")]
        s_xld=[sem("xT_loaded_0"),sem("xT_loaded_1")]; s_yst=[[sem(f"y{q}_stored_{l}") for l in range(2)] for q in range(2)]
        s_fw=sem("layer0_weights_loaded"); s_w2=sem("layer1_weights_loaded"); s_one=sem("ones_rows_ready")
        def need(eng,B,steps,i,*names,gate=False):
            for e,sm in (("pe",B.pe),("act",B.act),("dve",B.dve)):
                at=[steps[e].index(nm.split(":")[1]) for nm in names if nm.split(":")[0]==e]
                if at: eng.wait_ge(sm,i*len(steps[e])+max(at)+1+(B.first if e=="dve" else 0))
        def ended(eng,L,steps,iters):
            for B in L:
                for e,sm in (("pe",B.pe),("act",B.act),("dve",B.dve)):
                    eng.wait_ge(sm,iters*len(steps[e])+(B.first if e=="dve" else 0))
        def four(t): return t.rearrange("p (a b) -> p a b",a=4)
        fin=sb("final_rows",[P,3,16]); flagt=sb("overflow_flag",[P,2]); flag_i=sb("overflow_flag_i",[P,1],I32)
        fa_=bump(C0,D0); agg=fa_([NT,16]); asq=fa_([NT,16]); sc8=fa_([NT,8]); m8=fa_([NT,8]); mi8=fa_([NT,8],U32); mf2=fa_([NT,2]); dd=fa_([NT]); w12=fa_([NT,2])
        q4=fa_([2*NT,4]).rearrange("p (k n) e -> p k n e",k=2); wf4=fa_([NT,4]); yb=[fa_([8,4*D]),fa_([8,4*D])]; yt=fa_([8,4*D])
        s_th=sem("gate_difference_ready"); s_tw=sem("gate_tanh_ready"); s_yl=[sem("y_loaded_0"),sem("y_loaded_1")]; s_yu=sem("y_used"); s_fn=sem("tokens_ready")
        ov=bump(C0,D0); o_dst=ov([EC],I32); o_src=ov([EC],I32); o_rank=ov([EC]); o_key=ov([EC]); o_keyi=ov([EC],I32)
        oix=ov([3],I32); okey=ov([1]); orow=ov([3,ROW]); osc=ov([4]); odg=ov([5,P]); osel=ov([P]); oneg=ov([P]); otm=ov([4,P])
        onm=ov([4]); oex=ov([2,4]); owv=ov([20]); ost=ov([ROW])
        s_fl=sem("overflow_flag_ready"); s_fp=sem("overflow_flag_summed"); s_ol=sem("overflow_arrays_loaded"); s_osd=sem("state_stored"); s_orl=sem("state_reloaded")
        s_of=sem("overflow_keys"); s_od=sem("overflow_dve_step"); s_og=[sem(f"overflow_rows_gathered_{k}") for k in range(3)]; s_op=sem("overflow_pe_step"); s_oa=sem("overflow_exp"); s_osc=sem("overflow_scattered"); s_ogt=sem("overflow_pool_gate")
        state4=state_d.rearrange("(n p) f -> p n f",p=P)
        s_fin=sem("final_rows_loaded"); s_ya=sem("y_added"); s_ci=sem("column_numbers_ready")
        block=ctx.enter_context(nc.Block())
        bk_rows=buck.rearrange("(p c) o -> p (c o)",p=P)
        rows3=rows_e.rearrange("(p c) f -> p c f",p=P); sums3=sums_d.rearrange("(p c) f -> p c f",p=P)
        x4=xTd.rearrange("(n p) t -> p n t",p=D); y4=yd.rearrange("(n p) (q f) -> p n q f",p=P,q=2)

        @block.sync
        def _(sp):
            sp.dma_start(dst_i, edges[1].rearrange("(p c) -> p c",p=P)).then_inc(s_ld,16)
            sp.dma_start(src_i, edges[0].rearrange("(p c) -> p c",p=P)).then_inc(s_ld,16)
            sp.dma_start(fin[:,:,:],fin_d).then_inc(s_fin,16)
            sp.wait_ge(s_sent,1)
            sp.dma_start(bk_rows, sent).then_inc(s_fill,16)
            sp.wait_ge(s_z,1)
            for q,(d,s) in enumerate([(embT[:,:],embT_d),(w1T[:,:],w1T_d),(w2T[:,:],w2T_d),(tb1[:,:],tb1_d),(rows[:,:,:],rows_d),
                      (raw[0:D,:,0:D],proj_d),(raw[D:P,:,D:P],proj_d),(lora[0:D,:,0:D],lora_d),(lora[D:P,:,D:P],lora_d),
                      (vraw[:,:],wv_d),(graw[0:D,0,:],ag_d),(graw[D:P,1,:],ag_d),(bg[:,:],bg_d),(wo[0:D,0,:],wo_d),(wo[D:P,1,:],wo_d),(cols[:,0:11],cols_d)]):
                sp.dma_start(d,s).then_inc(s_w,16)
            sp.wait_ge(s_rk,1)
            sp.dma_start(rank_d, rank_f).then_inc(s_rks,16)
            xr=x.rearrange("(j b) t -> j (b t)",b=2)
            with sp.Fori(0,ITERS) as i:
                for l in range(LANES):
                    sp.wait_ge(L[l].dve,i*len(DVE_STEPS)+1)
                    sp.dma_start(L[l].tk[:,:], xr[bass.ds(i*LANES+l,1),:].broadcast_to((P,512))).then_inc(L[l].ld,16)
            for l in range(LANES):
                sp.wait_ge(L[l].dve,ITERS*len(DVE_STEPS)+1); sp.wait_ge(L[l].pe,ITERS*len(PE_STEPS)); sp.wait_ge(L[l].act,ITERS*len(ACT_STEPS))
            for dst,src in [(fgam[:,:,:],gam_d),(fwr[0:D+1],wr_d),(fw1[0:D],w1_d),(fb1[:,:],b1_d),(fw2[:,:,:],w2_d),(fb2[0:8],b2_d)]:
                sp.dma_start(dst,src).then_inc(s_fw,16)
            ended(sp,FL,F_STEPS,GI)
            for dst,src in [(aw[0:D+1],qkv_d),(ap[0:D+1],proj1_d),(gw[0:D],wg_d),(gatt,att_d),(lw1[0:D],lw1_d),(lb1,lb1_d),(lw2,lw2_d),(lb2,lb2_d)]:
                sp.dma_start(dst,src).then_inc(s_w2,16)
            x4=xTd.rearrange("(n p) t -> p n t",p=D)
            t4=tbl.rearrange("(n p) f -> p n f",p=P)
            with sp.Fori(0,GI) as i:
                for l in range(2):
                    need(sp,GL[l],G_STEPS,i,"act:xTs")
                    sp.dma_start(x4[:,bass.ds(i*2+l,1),:],GL[l].xT[0:D].unsqueeze(1)).then_inc(s_xst[l],16)
                    need(sp,GL[l],G_STEPS,i,"dve:rd")
                    sp.dma_start(t4[:,bass.ds((i*2+l)*4,4),:],GL[l].row).then_inc(s_tst[l],16)
            ended(sp,GL,G_STEPS,GI)
            for l in range(2): sp.wait_ge(s_xst[l],16*GI); sp.wait_ge(s_tst[l],16*GI)
            def store_rows(i):
                for g in range(2):
                    sp.wait_ge(s_gat[g],256*(i+1))
                    sp.dma_start(rows3[:,bass.ds(i*32+g*16,16),:], gs[:,g,:,:]).then_inc(s_row[g],16)
            def y_load(i,first):
                for l in range(2):
                    if not first: need(sp,YL[l],Y_STEPS,i-1,"pe:h3")
                    sp.dma_start(YL[l].xT[0:D].unsqueeze(1),x4[:,bass.ds(i*2+l,1),:]).then_inc(s_xld[l],16)
            def y_store(i):
                for q in range(2):
                    for l in range(2):
                        need(sp,YL[l],Y_STEPS,i,f"dve:b{q}")
                        sp.dma_start(y4[:,bass.ds((i*2+l)*4,4),q,:],four(YL[l].ys[:,q,:])).then_inc(s_yst[q][l],16)
            def both(i,first):
                y_load(i,first)
                for u in range(GPY): store_rows(i*GPY+u)
                y_store(i)
            both(0,True)
            with sp.Fori(1,GI-1) as i:
                both(i,False)
            y_load(GI-1,False)
            for u in range(GN-(GI-1)*GPY): store_rows((GI-1)*GPY+u)
            y_store(GI-1)
            for q in range(2):
                for l in range(2): sp.wait_ge(s_yst[q][l],16*GI)
            ended(sp,YL,Y_STEPS,GI)
            for g in range(2):
                sp.wait_ge(s_row[g],16*GN)
            for c in range(NCH):
                if c>=2:
                    sp.wait_ge(s_sum,c-1)
                    sp.dma_start(sums3[:,(c-2)*CH:(c-1)*CH,:], rch[:,c%2,:,:]).then_inc(s_sst[c%2],16)
                    sp.wait_ge(s_sst[c%2],16*(c//2))
                sp.dma_start(rch[:,c%2,:,:], rows3[:,c*CH:(c+1)*CH,:]).then_inc(s_rld[c%2],16)
            for c in range(NCH,NCH+2):
                sp.wait_ge(s_sum,c-1)
                sp.dma_start(sums3[:,(c-2)*CH:(c-1)*CH,:], rch[:,c%2,:,:]).then_inc(s_sst[c%2],16)
            sp.wait_ge(s_eg,16*P); sp.wait_ge(s_fl,2)
            over=sp.value_load(flag_i[0:1,0:1],min_val=0,max_val=P)
            with sp.If(over>0):
                sp.dma_start(state4,ends).then_inc(s_osd,16)
                sp.dma_start(o_dst, edges[1].rearrange("(p c) -> p c",p=P)).then_inc(s_ol,16)
                sp.dma_start(o_src, edges[0].rearrange("(p c) -> p c",p=P)).then_inc(s_ol,16)
                sp.wait_ge(s_rks,16)
                sp.dma_start(o_rank, rank_d).then_inc(s_ol,16)
                sp.wait_ge(s_osd,16); sp.wait_ge(s_osc,16*EC)
                sp.dma_start(ends,state4).then_inc(s_orl,16)
                sp.wait_ge(s_orl,16)
            sp.wait_ge(s_th,1)
            yv=yd.rearrange("(n p) f -> p n f",p=P)
            def y_in(i,first):
                for b in range(2):
                    if not first: sp.wait_ge(s_yu,2*i+b-1)
                    sp.dma_start(yb[b],yv[:,bass.ds((i*2+b)*8,8),:]).then_inc(s_yl[b],16)
            y_in(0,True)
            with sp.Fori(1,NT//16) as i:
                y_in(i,False)
            sp.wait_ge(s_fn,1)
            sp.dma_start(out.rearrange("(n p) f -> p n f",p=P), H[:,:,:]).then_inc(s_out,16)
            sp.wait_ge(s_out,16); sp.wait_ge(s_rks,16)

        @block.gpsimd
        def _(pool):
            G=nc.gpsimd; n=[0]
            def lk(ins):
                n[0]+=1; ins.then_inc(s_g,1); pool.wait_ge(s_g,n[0])
            lk(G.iota(iota_i[:,:], pattern=[[1,P]], base=0, channel_multiplier=0))
            lk(G.iota(rowp_i[:,:], pattern=[[0,1]], base=0, channel_multiplier=1))
            lk(G.memset(dumi[:,:],0.0))
            lk(G.memset(zero_b[:,:],0.0))
            lk(G.memset(ones_b[:,:],1.0))
            lk(G.affine_select(out=tri[:,:],in_=ones_b[:,:],compare_op=ALU.is_gt,fill=0.0,base=0,pattern=[[1,P]],channel_multiplier=-1))
            G.affine_select(out=anti[:,:],in_=ones_b[:,:],compare_op=ALU.is_ge,fill=0.0,base=0,pattern=[[-1,P]],channel_multiplier=1).then_inc(s_const,1)
            pool.wait_ge(s_const,1)
            lk(G.iota(iot_i[:,:],pattern=[[1,8]],base=0,channel_multiplier=0))
            lk(G.iota(mk_i[:,:],pattern=[[0,2]],base=0,channel_multiplier=1))
            G.memset(ones_f[:,:],1.0).then_inc(s_mc,1)
            pool.wait_ge(s_mc,1)
            lk(G.memset(raw[:,:,:],0.0))
            lk(G.memset(graw[:,:,:],0.0)); lk(G.memset(wo[:,:,:],0.0)); G.memset(lora[:,:,:],0.0).then_inc(s_z,1)
            pool.wait_ge(s_z,1)
            lk(G.iota(ip_i[:,:],pattern=[[P,2]],base=0,channel_multiplier=1))
            lk(G.memset(onesblk[:,:],0.0));
            lk(G.memset(flag[:,:],1.0))
            lk(G.memset(onesblk[0:D,0:D],1.0)); lk(G.memset(onesblk[D:P,D:P],1.0))
            lk(G.memset(flag.rearrange("p (c t) -> p c t",c=NC)[:,:,0:1],0.0))
            aff=lambda o,pat,mult,base,op: G.affine_select(out=o,in_=ones_f[0:o.shape[0],0:64] if len(o.shape)==2 and o.shape[1]==64 else ones_f[:,:],compare_op=op,fill=0.0,base=base,pattern=pat,channel_multiplier=mult)
            lk(aff(ident[:,:],[[1,P]],-1,0,ALU.is_equal))
            lk(aff(mrep[:,0,:],[[1,D]],-1,0,ALU.is_gt))
            lk(aff(mrep[:,1,:],[[1,D]],-1,0,ALU.is_ge))
            lk(aff(mrep[:,2,:],[[-1,D]],1,0,ALU.is_gt))
            lk(G.iota(jb_i[:,:],pattern=[[1,4],[0,16]],base=0,channel_multiplier=0))
            G.iota(pb_i[:,:],pattern=[[0,1]],base=0,channel_multiplier=1).then_inc(s_c,1)
            pool.wait_ge(s_c,1)
            pool.wait_ge(s_fill,16)
            def slot(g,k,copies,waits):
                for sm,v in waits: pool.wait_ge(sm,v)
                G.tensor_tensor(dumi[:,1:2],dumi[:,0:1],dumi[:,0:1],ALU.add).then_inc(s_gate,1)
                pool.wait_ge(s_gate,3*k+1)
                for o,s in copies: last=G.tensor_copy(o,s)
                last.then_inc(s_gate,1)
                pool.wait_ge(s_gate,3*k+2)
                G.tensor_tensor(dumi[:,2:3],dumi[:,0:1],dumi[:,0:1],ALU.add).then_inc(s_gate,1)
            def scatter(i,first):
                for g in range(2):
                    at=bass.ds(i*32+g*16,16)
                    slot(g,2*i+g,[(idx16[:,g,:],idx_all[:,at]),(key16[:,g,:],key_all[:,at])],[(s_stage,2*i+g+1)]+([] if first else [(s_scat[g],256*i)]))
                    for c in range(16):
                        G.indirect_dma_start(out=buck, out_offset=bass.IndirectOffsetOnAxis(ap=idx16[:,g,c:c+1],axis=0),
                            in_=key16[:,g,c:c+1], in_offset=None, bounds_check=P*EW-1, oob_is_err=False).then_inc(s_scat[g],16)
            scatter(0,True)
            with G.Fori(1,EC//32) as i:
                scatter(i,False)
            for g in range(2): pool.wait_ge(s_scat[g],16*EC//2)
            G.dma_start(K[0][:,P:SW], bk_rows).then_inc(s_bk,16)
            for l in range(LANES): pool.wait_ge(L[l].dve,ITERS*len(DVE_STEPS)+1); pool.wait_ge(L[l].pe,ITERS*len(PE_STEPS)); pool.wait_ge(L[l].act,ITERS*len(ACT_STEPS))
            G.iota(col_i, pattern=[[-1,SW]], base=4096, channel_multiplier=0).then_inc(s_ci,1)
            pool.wait_ge(s_gi,1)
            ended(pool,GL,G_STEPS,GI)
            for l in range(2): pool.wait_ge(s_tst[l],16*GI)
            def gather(i,first):
                for g in range(2):
                    slot(g,2*i+g+EC//16,[(gidx16[:,g,:],gidx[:,bass.ds(i*32+g*16,16)])],[] if first else [(s_row[g],i*16),(s_acp,2*i+g-1)])
                    for c in range(16):
                        G.indirect_dma_start(out=gs[:,g,c,:], out_offset=None, in_=tbl,
                            in_offset=bass.IndirectOffsetOnAxis(ap=gidx16[:,g,c:c+1],axis=0)).then_inc(s_gat[g],16)
            gather(0,True)
            with G.Fori(1,GN) as i:
                gather(i,False)
            pool.wait_ge(s_ei,1)
            for g in range(2):
                pool.wait_ge(s_sst[g],16*(NCH//2))
            for c in range(P):
                G.indirect_dma_start(out=ends[:,c,:], out_offset=None, in_=sums_d,
                    in_offset=bass.IndirectOffsetOnAxis(ap=end_i[:,c:c+1],axis=0)).then_inc(s_eg,16)
            pool.wait_ge(s_fl,2)
            over=pool.value_load(flag_i[0:1,0:1],min_val=0,max_val=P)
            with pool.If(over>0):
                pool.wait_ge(s_osd,16)
                G.tensor_tensor(dumi[:,1:2],dumi[:,0:1],dumi[:,0:1],ALU.add).then_inc(s_ogt,1)
                with G.Fori(0,EC) as i:
                    pool.wait_ge(s_od,i*O_STEPS+1); pool.wait_ge(s_ogt,2*i+1)
                    G.tensor_tensor(dumi[:,1:2],dumi[:,0:1],dumi[:,0:1],ALU.add).then_inc(s_ogt,1)
                    for k,(src,c) in enumerate([(tbl,0),(tbl,1),(state_d,1)]):
                        G.indirect_dma_start(out=orow[:,k,:], out_offset=None, in_=src,
                            in_offset=bass.IndirectOffsetOnAxis(ap=oix[:,c:c+1],axis=0)).then_inc(s_og[k],16)
                    pool.wait_ge(s_od,i*O_STEPS+O_STEPS); pool.wait_ge(s_ogt,2*i+2)
                    G.tensor_tensor(dumi[:,1:2],dumi[:,0:1],dumi[:,0:1],ALU.add).then_inc(s_ogt,1)
                    G.indirect_dma_start(out=state_d, out_offset=bass.IndirectOffsetOnAxis(ap=oix[:,2:3],axis=0),
                        in_=ost, in_offset=None, bounds_check=M-1, oob_is_err=False).then_inc(s_osc,16)

        @block.tensor
        def _(pe):
            mm=lambda o,a,b,st=True,sp_=True: nc.tensor.matmul(o,a,b,start=st,stop=sp_,skip_group_check=True)
            mb=lambda o,l,r,st=False: nc.tensor.matmul(o,l,r,start=st,stop=False,skip_group_check=True)
            PS0=PS[0][:,:].rearrange("p (u e) -> p u e",u=4)
            rep=lambda s,u,k: oh[:,s,u:u+1,:].broadcast_to((P,k,P))
            pe.wait_ge(s_const,1)
            pe.wait_ge(s_oh,1)
            mb(PS0,zero_b[:,:],oh[:,0,:,:],True).then_inc(s_post,1)
            with pe.Fori(0,EC//8) as i:
                for s in range(2):
                    k=2*i+s
                    pe.wait_ge(s_oh,k+1)
                    for u in range(3):
                        mb(PS0[:,u+1:4,:],ones_b[:,:],rep(s,u,3-u))
                    mb(PS0,tri[:,:],oh[:,s,:,:]).then_inc(s_pre,1)
                    pe.wait_ge(s_rd,k+1)
                    for u in range(1,4):
                        mb(PS0[:,0:u,:],ones_b[:,:],rep(s,u,u))
                    mb(PS0,anti[:,:],oh[:,s,:,:]).then_inc(s_post,1)
            pe.wait_ge(s_rd,EC//4); pe.wait_ge(s_bn,1)
            ps0=L[0].ps
            pe.wait_ge(s_w,16*16)
            mm(ps0[0][0:D,0:256],w1T[:,:],embT[:,:]).then_inc(s_t,1)
            pe.wait_ge(s_ta,1)
            for v in range(2):
                r=mm(ps0[1][:,v*D:(v+1)*D],hT[:,v*P:(v+1)*P],w2T[:,:])
            r.then_inc(s_t,1)
            pe.wait_ge(s_tt,1)
            pe.wait_ge(s_c,1)
            wait=mk(pe,"pe")
            def it(i):
                def step(fn):
                    for l in range(LANES):
                        B=L[l]
                        r=fn(l,B,lambda *n: wait(l,i,*n))
                        r.then_inc(B.pe,1)
                def xg(l,B,w):
                    w("dve:oneh")
                    for h,s in halves:
                        for v in range(2):
                            r=mm(B.ps[0][s,0:T],tab[:,v,0:D],B.oneh[:,v,h*T:(h+1)*T],v==0,v==1)
                    return r
                step(xg)
                def h0(l,B,w):
                    for t in range(4):
                        for v in range(2):
                            r=mm(B.ps[1][:,t*D:(t+1)*D],B.oneh[:,v,t*P:(t+1)*P],tab[:,v,D:2*D],v==0,v==1)
                    return r
                step(h0)
                def proj(l,B,w):
                    w("act:xs")
                    for q in range(4):
                        o=B.ps[q//2][:,(q%2)*T:(q%2+1)*T]
                        mm(o,wx[:,q,:],B.x[:,1:257],True,False); r=mm(o,ws[:,q,:],B.x[:,0:256],False,True)
                    return r
                step(proj)
                def glin(l,B,w):
                    for h,s in halves:
                        o=B.ps[2][:,h*T:(h+1)*T]
                        mm(o,gx[:,h,:],B.x[:,1:257],True,False); r=mm(o,gsf[:,h,:],B.x[:,0:256],False,True)
                    return r
                step(glin)
                def vtok(l,B,w):
                    for c in range(4):
                        for h,s in halves:
                            o=B.ps[3][s,c*D:(c+1)*D]
                            mm(o,B.x[s,1+c*D:1+c*D+D],vx[s,:],True,False); r=mm(o,B.x[s,c*D:c*D+D],vs[s,:],False,True)
                    return r
                step(vtok)
                def zz(l,B,w):
                    w("act:th","act:za")
                    mm(B.ps[1][:,0:T],lora[:,0,:],B.th[:,:]); return mm(B.ps[1][:,T:2*T],lora[:,1,:],B.za[:,:])
                step(zz)
                def ss(l,B,w):
                    w("act:sq","act:sgt")
                    return mm(B.ps[2][:,0:T],onesblk[:,:],B.sq[:,:])
                step(ss)
                def each(o,a,b,l,B):
                    for c in range(4):
                        for h,s in halves:
                            r=mm(o(c)[s],a(c)[s],b(c)[s])
                    return r
                def BKt(l,B,w):
                    w("act:tw","act:ta","dve:B","dve:K")
                    each(lambda c:B.ps[1][:,c*D:(c+1)*D],lambda c:B.B[:,c*D:(c+1)*D],lambda c:idh,l,B)
                    return each(lambda c:B.ps[1][:,T+c*D:T+(c+1)*D],lambda c:B.K[:,c*D:(c+1)*D],lambda c:idh,l,B)
                step(BKt)
                def At(l,B,w):
                    w("act:V","dve:A")
                    return each(lambda c:B.ps[3][:,c*D:(c+1)*D],lambda c:B.AR[:,c,0,:],lambda c:idh,l,B)
                step(At)
                def gtk(l,B,w):
                    w("dve:sg","dve:ssm")
                    for c in range(4):
                        for h,s in halves:
                            r=mm(B.ps[2][s,T+c*D:T+(c+1)*D],B.sg[:,h,c*D:(c+1)*D],bg[:,:])
                    return r
                step(gtk)
                def bon(l,B,w):
                    w("dve:rk","act:Ats")
                    for c in range(4):
                        for h,s in halves:
                            r=mm(B.ps[3][s,T+c:T+c+1],B.rk[s,c*D:(c+1)*D],col("r_k")[s])
                    return r
                step(bon)
                def G1(l,B,w):
                    w("dve:kq","dve:R","dve:rk")
                    return each(lambda c:B.ps[0][:,c*P:(c+1)*P],lambda c:B.B[:,c*D:(c+1)*D],lambda c:B.AR[:,c,:,:].rearrange("p a b -> p (a b)"),l,B)
                step(G1)
                def G2(l,B,w):
                    w("dve:ssm","act:gts")
                    return each(lambda c:B.ps[2][:,c*P:(c+1)*P],lambda c:B.K[:,c*D:(c+1)*D],lambda c:B.AR[:,c,:,:].rearrange("p a b -> p (a b)"),l,B)
                step(G2)
                def Lm(l,B,w):
                    w("act:BKs")
                    return each(lambda c:B.ps[1][:,c*D:(c+1)*D],lambda c:B.AR[:,c,0,:],lambda c:B.B[:,c*D:(c+1)*D],l,B)
                step(Lm)
                def p2(l,B,w):
                    w("dve:g1","dve:l","act:Ats","act:bons")
                    each(lambda c:B.ps[3][:,c*D:(c+1)*D],lambda c:B.g1[:,c,0,:],lambda c:B.lo[:,0,c,:],l,B)
                    return each(lambda c:B.ps[3][:,T+c*D:T+(c+1)*D],lambda c:B.lo[:,0,c,:],lambda c:B.g1[:,c,0,:],l,B)
                step(p2)
                def x2(l,B,w):
                    w("act:p2s","dve:d1")
                    return each(lambda c:B.ps[0][:,c*D:(c+1)*D],lambda c:B.pp[:,0,c,:],lambda c:B.dta[:,c,:],l,B)
                step(x2)
                def p4(l,B,w):
                    w("dve:g2")
                    each(lambda c:B.ps[2][:,c*D:(c+1)*D],lambda c:B.pp[:,1,c,:],lambda c:B.pp[:,0,c,:],l,B)
                    return each(lambda c:B.ps[2][:,T+c*D:T+(c+1)*D],lambda c:B.pp[:,0,c,:],lambda c:B.pp[:,1,c,:],l,B)
                step(p4)
                def x4(l,B,w):
                    w("act:p4s","dve:d2")
                    return each(lambda c:B.ps[0][:,T+c*D:T+(c+1)*D],lambda c:B.p4[:,0,c,:],lambda c:B.dtb[:,c,:],l,B)
                step(x4)
                def p8(l,B,w):
                    w("dve:o")
                    return each(lambda c:B.ps[1][:,c*D:(c+1)*D],lambda c:B.p4[:,1,c,:],lambda c:B.p4[:,0,c,:],l,B)
                step(p8)
                def x8(l,B,w):
                    w("act:p8s","dve:d4")
                    return each(lambda c:B.ps[1][:,T+c*D:T+(c+1)*D],lambda c:B.p8[:,c,:],lambda c:B.dta[:,c,:],l,B)
                step(x8)
                def EE(l,B,w):
                    w("dve:d8","act:p2s")
                    each(lambda c:B.ps[3][:,c*D:(c+1)*D],lambda c:B.dtb[:,c,:],lambda c:B.lo[:,1,c,:],l,B)
                    return each(lambda c:B.ps[3][:,T+c*D:T+(c+1)*D],lambda c:B.lo[:,1,c,:],lambda c:B.dtb[:,c,:],l,B)
                step(EE)
                def MKV(l,B,w):
                    return each(lambda c:B.ps[0][:,c*D:(c+1)*D],lambda c:B.g2[:,c,0,:],lambda c:B.V[:,c,:],l,B)
                step(MKV)
                def E2(l,B,w):
                    w("act:EEs","act:MKVs")
                    return each(lambda c:B.ps[0][:,T+c*D:T+(c+1)*D],lambda c:B.EE[:,0,c,:],lambda c:B.EE[:,1,c,:],l,B)
                step(E2)
                f2=lambda t: (lambda c: t[:,c,:,:].rearrange("p a b -> p (a b)"))
                def Z0(l,B,w):
                    w("act:MKVs")
                    return each(lambda c:B.ps[2][:,c*P:(c+1)*P],lambda c:B.dtb[:,c,:],f2(B.YA),l,B)
                step(Z0)
                def Z1(l,B,w):
                    w("act:Z0s","act:E2s")
                    return each(lambda c:B.ps[1][:,c*P:(c+1)*P],lambda c:B.E2[:,c,:],f2(B.Z0),l,B)
                step(Z1)
                def Wf(l,B,w):
                    w("dve:Z1")
                    return each(lambda c:B.ps[3][:,c*P:(c+1)*P],lambda c:B.EE[:,1,c,:],f2(B.Z1),l,B)
                step(Wf)
                def W1T(l,B,w):
                    w("dve:W")
                    return each(lambda c:B.ps[0][:,c*D:(c+1)*D],lambda c:B.Wy[:,c,1,:],lambda c:idh,l,B)
                step(W1T)
                uu=lambda B,c: (B.Wy[:,0,0,:] if c==0 else B.U[:,c,:])
                for c in range(4):
                    if c:
                        def U(l,B,w):
                            w("act:W1Ts",f"act:S{c}")
                            for h,s in halves: r=mm(B.ps[2][s,c*D:(c+1)*D],B.W1T[s,c,:],B.S[s,c,:])
                            return r
                        step(U)
                    if c<3:
                        def Sp(l,B,w):
                            if c: w(f"dve:U{c}")
                            for h,s in halves:
                                o=B.ps[1][s,c*D:(c+1)*D]
                                mm(o,B.BK[s,0,c,:],uu(B,c)[s],True,False)
                                r=mm(o,B.BK[s,1,c,:],B.V[s,c,:],False,c==0)
                                if c: r=mm(o,idh[s],B.S[s,c,:],False,True)
                            return r
                        step(Sp)
                    def Oc(l,B,w):
                        if c==3: w("dve:U3")
                        for h,s in halves:
                            o=B.ps[3][s,c*D:(c+1)*D]
                            mm(o,B.g1[s,c,1,:],uu(B,c)[s],True,False)
                            r=mm(o,B.g2[s,c,1,:],B.V[s,c,:],False,c==0)
                            if c: r=mm(o,B.AR[s,c,1,:],B.S[s,c,:],False,True)
                        return r
                    step(Oc)
                def yT(l,B,w):
                    w("dve:og")
                    return each(lambda c:B.ps[2][:,T+c*D:T+(c+1)*D],lambda c:B.oc[:,c,:],lambda c:idh,l,B)
                step(yT)
                def wof(l,B,w):
                    w("act:yTs")
                    for t in range(2):
                        r=mm(B.ps[0][:,T+t*P:T+(t+1)*P],B.yT[:,t*P:(t+1)*P],wo[:,:,:].rearrange("p h d -> p (h d)"))
                    return r
                step(wof)
            idh=i64
            with pe.Fori(0,ITERS) as i:
                it(i)
            for l in range(LANES): pe.wait_ge(L[l].dve,ITERS*len(DVE_STEPS)+1)
            pe.wait_ge(s_mc,1); pe.wait_ge(s_fw,16*6)
            pe.wait_ge(s_one,1)
            with pe.Fori(0,GI) as i:
                def step(fn,*names):
                    for B in FL:
                        need(pe,B,F_STEPS,i,*names)
                        fn(B).then_inc(B.pe,1)
                def xT(B):
                    for t in range(4): r=mm(B.ps[3][0:D,t*P:(t+1)*P],B.xs[:,t,:],ident[:,:])
                    return r
                step(xT,"dve:xb")
                def lg(B):
                    for t in range(4): r=mm(B.ps[3][:,t*8:(t+1)*8],B.xT[0:D+1,t*P:(t+1)*P],fwr[0:D+1])
                    return r
                step(lg,"act:xTs")
                h=lambda e: (lambda B: mm(B.ps[e%2][:,:],fw1[0:D,e,:],B.xT[0:D]))
                step(h(0)); step(h(1))
                for e in range(8):
                    def y(B):
                        for t in range(4): r=mm(four(B.ps[2][:,:])[:,t,(e%2)*D:(e%2+1)*D],B.hT[:,e%2,t*P:(t+1)*P],fw2[:,e,:])
                        return r
                    step(y,f"act:g{e}",*([f"dve:ym{e//2-1}"] if e>=2 and e%2==0 else []))
                    if e<6: step(h(e+2))
                def wT(B):
                    for t in range(4): r=mm(B.ps[3][0:8,t*P:(t+1)*P],B.wf[:,t,:],ident[:,:])
                    return r
                step(wT,"dve:wf")
                def bias(B):
                    for t in range(4): r=mm(B.ps[3][:,t*D:(t+1)*D],B.wTs[0:8,t*P:(t+1)*P],fb2[0:8])
                    return r
                step(bias,"act:wTs")
            ended(pe,FL,F_STEPS,GI)
            pe.wait_ge(s_w2,16*8)
            with pe.Fori(0,AI) as i:
                def step(fn,*names):
                    for B in AL:
                        need(pe,B,A_STEPS,i,*names)
                        fn(B).then_inc(B.pe,1)
                def xT(B):
                    pe.wait_ge(B.dve,i*len(A_STEPS["dve"])+1)
                    return mm(B.ps[0][0:D,0:P],B.xs,ident[:,:])
                step(xT,"act:xs")
                def qkv(B):
                    for h,s in HALVES:
                        w=slice(h*D,(h+1)*D)
                        mm(B.ps[0][s,P:P+D],aw[0:D+1,0:D],B.xT[0:D+1,w])
                        mm(B.ps[0][s,P+D:2*P],aw[0:D+1,D:2*D],B.xT[0:D+1,w])
                        for _,s2 in HALVES: r=mm(B.ps[0][s2,2*P+h*D:2*P+(h+1)*D],B.xT[0:D+1,w],aw[0:D+1,2*D:3*D])
                    return r
                step(qkv,"act:xTs")
                step(lambda B: mm(B.ps[1][:,:],B.Q,B.K.rearrange("p h j -> p (h j)")),"act:q","dve:kb")
                def PT(B):
                    for g in range(4): r=mm(B.ps[1][:,g*P:(g+1)*P],B.E[:,2*g:2*g+2,:].rearrange("p a b -> p (a b)"),ident[:,:])
                    return r
                step(PT,"act:ex","dve:sb")
                def pv(B):
                    for h,s in HALVES:
                        for g in range(4):
                            r=mm(B.ps[0][s,384+g*16:384+(g+1)*16],B.PT[:,g,h*D:(h+1)*D],B.V[:,h,g*16:(g+1)*16])
                    return r
                step(pv,"act:PTs","dve:vb")
                step(lambda B: mm(B.ps[0][0:D,0:P],B.o,ident[:,:]),"dve:on")
                step(lambda B: mm(B.ps[0][:,448:512],B.oT[0:D+1],ap[0:D+1]),"act:oTs")
            ended(pe,AL,A_STEPS,AI)
            with pe.Fori(0,GI) as i:
                def step(fn,*names):
                    for B in GL:
                        need(pe,B,G_STEPS,i,*names)
                        fn(B).then_inc(B.pe,1)
                def xT(B):
                    for t in range(4): r=mm(B.ps[0][0:D,t*P:(t+1)*P],B.xs[:,t,:],ident[:,:])
                    return r
                step(xT,"act:xs")
                def hg(B):
                    for t in range(4): r=mm(B.ps[1][:,t*16:(t+1)*16],B.xT[0:D,t*P:(t+1)*P],gw[0:D])
                    return r
                step(hg,"act:xTs")
            ended(pe,GL,G_STEPS,GI)
            with pe.Fori(0,GI) as i:
                def h(e,B): return mm(B.ps[e%2][:,:],lw1[0:D,e,:],B.xT[0:D])
                def y(e,B):
                    for t in range(4): r=mm(four(B.ps[2+e//2][:,:])[:,t,(e%2)*D:(e%2+1)*D],B.hT[:,e%2,t*P:(t+1)*P],lw2[:,e,:])
                    return r
                for k,e in [("h",0),("h",1),("y",0),("h",2),("y",1),("h",3),("y",2),("y",3)]:
                    for l,B in enumerate(YL):
                        if k=="h":
                            if e==0: pe.wait_ge(s_xld[l],16*i+16)
                            h(e,B).then_inc(B.pe,1)
                        else:
                            need(pe,B,Y_STEPS,i,f"act:g{e}")
                            y(e,B).then_inc(B.pe,1)
            pe.wait_ge(s_fl,1)
            mm(PS[7][0:1,0:1],flagt[:,1:2],ones_f[:,0:1]).then_inc(s_fp,1)
            pe.wait_ge(s_fl,2)
            over=pe.value_load(flag_i[0:1,0:1],min_val=0,max_val=P)
            with pe.If(over>0):
                with pe.Fori(0,EC) as i:
                    pe.wait_ge(s_od,i*O_STEPS+5)
                    mm(PS[6][:,0:P],ones_f[:,:],odg[:,0,:])
                    mm(PS[7][:,:],ones_f[:,:],odg[:,1:5,:].rearrange("p a b -> p (a b)")).then_inc(s_op,1)
                    pe.wait_ge(s_od,i*O_STEPS+14)
                    mm(PS[6][:,P:P+20],osel,owv).then_inc(s_op,1)

        @block.scalar
        def _(act):
            A=nc.scalar
            act.wait_ge(s_t,1)
            A.activation(hT[:,:],L[0].ps[0][0:D,0:256],ACT.Relu,bias=tb1[:,0:1]).then_inc(s_ta,1)
            for k in range(2):
                act.wait_ge(s_tv,k+1)
                A.activation(tst[:,0:2],tst[:,2:4],ACT.Ln).then_inc(s_ta,1)
                act.wait_ge(s_ta,2+2*k)
                A.activation(tst[:,0:2],tst[:,0:2],ACT.Exp,scale=-0.5).then_inc(s_ta,1)
            act.wait_ge(s_tt,1)
            wait=mk(act,"act")
            def it(i):
                def step(fn,*need):
                    for l in range(LANES):
                        wait(l,i,*need)
                        fn(L[l]).then_inc(L[l].act,1)
                step(lambda B:A.copy(B.h0[:,:,:],B.ps[1][:,0:T].rearrange("p (c t) -> p c t",c=4)),"pe:h0")
                step(lambda B:A.copy(B.x[:,1:257],B.ps[0][:,0:T]),"pe:xg")
                step(lambda B:A.copy(B.V[:,:,:],c4(B.ps[3][:,0:T])),"pe:vtok")
                step(lambda B:A.activation(B.th[:,:],B.ps[1][:,0:T],ACT.Tanh),"pe:proj")
                step(lambda B:A.copy(B.za[:,:],B.ps[1][:,T:2*T]),"pe:proj")
                step(lambda B:A.activation(B.sg[:,:,:],B.ps[2][:,:].rearrange("p (h t) -> p h t",h=2),ACT.Tanh,scale=0.5),"pe:glin")
                step(lambda B:A.activation(B.w[:,:],B.ps[1][:,0:T],ACT.Tanh,scale=0.5,bias=col("b_w2")),"pe:zz")
                step(lambda B:A.activation(B.a[:,:],B.ps[1][:,T:2*T],ACT.Tanh,scale=0.5,bias=col("b_a2")),"pe:zz")
                step(lambda B:A.activation(B.sq[:,:],B.ps[0][:,T:2*T],ACT.Square,scale=col("k_k")),"pe:proj")
                step(lambda B:A.activation(B.e1[:,:],B.cs[:,:],ACT.Exp),"dve:cs")
                step(lambda B:A.activation(B.e2[:,:],B.cm[:,:],ACT.Exp),"dve:cm")
                step(lambda B:A.activation(B.e3[:,:],B.cs[:,:],ACT.Exp,scale=-1.0),"dve:cs")
                step(lambda B:A.activation(B.rn[:,:],B.b0[:,:],ACT.Ln,scale=float(2**30)),"dve:ssm")
                step(lambda B:A.activation(B.rn[:,:],B.rn[:,:],ACT.Exp,scale=-0.5,bias=lnb[:,0:1]),"act:lnk")
                step(lambda B:A.copy(B.BK[:,:,:,:],B.ps[1][:,:].rearrange("p (k c t) -> p k c t",k=2,c=4)),"pe:BKt")
                step(lambda B:A.copy(B.YA[:,:,1,:],c4(B.ps[3][:,0:T])),"pe:At")
                step(lambda B:A.copy(B.gt[:,:,:],c4(B.ps[2][:,T:2*T])),"pe:gtk")
                step(lambda B:A.copy(B.bon[:,:],B.ps[3][:,T:T+4]),"pe:bon")
                step(lambda B:A.copy(B.pp[:,:,:,:],B.ps[3][:,:].rearrange("p (k c t) -> p k c t",k=2,c=4)),"pe:p2")
                step(lambda B:A.copy(B.p4[:,:,:,:],B.ps[2][:,:].rearrange("p (k c t) -> p k c t",k=2,c=4)),"pe:p4")
                step(lambda B:A.copy(B.p8[:,:,:],c4(B.ps[1][:,0:T])),"pe:p8")
                step(lambda B:A.copy(B.EE[:,:,:,:],B.ps[3][:,:].rearrange("p (k c t) -> p k c t",k=2,c=4)),"pe:EE")
                step(lambda B:A.copy(B.YA[:,:,0,:],c4(B.ps[0][:,0:T])),"pe:MKV")
                step(lambda B:A.copy(B.E2[:,:,:],c4(B.ps[0][:,T:2*T])),"pe:E2")
                step(lambda B:A.copy(B.Z0[:,:,:,:],B.ps[2][:,:].rearrange("p (c a t) -> p c a t",a=2,c=4)),"pe:Z0")
                step(lambda B:A.copy(B.W1T[:,:,:],c4(B.ps[0][:,0:T])),"pe:W1T")
                for c in range(3):
                    step(lambda B:A.activation(B.S[:,c+1,:],B.ps[1][:,c*D:(c+1)*D],ACT.Copy,scale=B.e1[:,(c+1)*D-1:(c+1)*D]),f"pe:Sp{c}")
                step(lambda B:A.copy(B.O[:,:,:],c4(B.ps[3][:,0:T])),"pe:O3")
                step(lambda B:A.activation(B.osq[:,:,:],B.oc[:,:,:],ACT.Square),"dve:oc")
                step(lambda B:A.activation(B.st[:,:,2],B.st[:,:,1],ACT.Ln,scale=1.0/D,bias=lnb[:,1:2]),"dve:var")
                step(lambda B:A.activation(B.st[:,:,3],B.st[:,:,2],ACT.Exp,scale=-0.5),"act:lnv")
                step(lambda B:A.copy(B.yT[:,:],B.ps[2][:,T:2*T]),"pe:yT")
            with act.Fori(0,ITERS) as i:
                it(i)
            for l in range(LANES): act.wait_ge(L[l].dve,ITERS*len(DVE_STEPS)+1)
            nl=[0]
            def norm_act(k):
                for c in range(2):
                    h=slice(c*D,(c+1)*D)
                    nl[0]+=1; act.wait_ge(s_la,nl[0])
                    A.activation(sq[:,h,:],xn[:,h,:],ACT.Square).then_inc(s_lb,1)
                    nl[0]+=1; act.wait_ge(s_la,nl[0])
                    A.activation(lst[:,2,h],lst[:,1,h],ACT.Ln,scale=1.0/D,bias=eps[:,0:1]).then_inc(s_lc,1)
                    act.wait_ge(s_lc,nl[0]//2)
                    A.activation(lst[:,3,h],lst[:,2,h],ACT.Exp,scale=-0.5).then_inc(s_lb,1)
            norm_act(0); norm_act(1)
            with act.Fori(0,GI) as i:
                def step(fn,*names):
                    for B in FL:
                        need(act,B,F_STEPS,i,*names)
                        fn(B).then_inc(B.act,1)
                step(lambda B:A.copy(B.xT[0:D],B.ps[3][0:D,:]),"pe:xT")
                step(lambda B:A.copy(B.lg.rearrange("p a b -> p (a b)"),B.ps[3][:,0:32]),"pe:lg")
                step(lambda B:A.activation(B.dd,B.dd,ACT.Tanh,scale=0.5),"dve:dd")
                for e in range(8):
                    step(lambda B:A.activation(B.hT[:,e%2,:],B.ps[e%2][:,:],ACT.Gelu,bias=fb1[:,e:e+1]),f"pe:h{e}")
                step(lambda B:A.copy(B.wTs[0:8],B.ps[3][0:8,:]),"pe:wT")
            ended(act,FL,F_STEPS,GI)
            norm_act(2)
            s_=slice
            with act.Fori(0,AI) as i:
                def step(fn,*names):
                    for l,B in enumerate(AL):
                        need(act,B,A_STEPS,i,*names)
                        fn(B,l).then_inc(B.act,1)
                def xs(B,l):
                    return A.copy(B.xs.unsqueeze(1),xn[:,bass.ds(i*4+l,1),:])
                step(xs)
                step(lambda B,l:A.copy(B.xT[0:D],B.ps[0][0:D,0:P]),"pe:xT")
                def q(B,l):
                    A.copy(B.Q[0:D,0:D],B.ps[0][0:D,P:P+D]); return A.copy(B.Q[D:P,D:P],B.ps[0][D:P,P:P+D])
                step(q,"pe:qkv")
                step(lambda B,l:A.activation(B.E,B.E,ACT.Exp,scale=8**-0.5),"dve:sb")
                step(lambda B,l:A.copy(B.PT.rearrange("p a b -> p (a b)"),B.ps[1][:,:]),"pe:PT")
                step(lambda B,l:A.copy(B.oT[0:D],B.ps[0][0:D,0:P]),"pe:oT")
            ended(act,AL,A_STEPS,AI)
            norm_act(3)
            def gat(i,first):
                def step(fn,*names):
                    for l,B in enumerate(GL):
                        need(act,B,G_STEPS,i,*names)
                        fn(B,l).then_inc(B.act,1)
                step(lambda B,l:A.copy(B.xs,xn[:,bass.ds((i*2+l)*4,4),:]))
                def xTs(B,l):
                    if not first: act.wait_ge(s_xst[l],16*i)
                    return A.copy(B.xT[0:D],B.ps[0][0:D,:])
                step(xTs,"pe:xT")
                def hgs(B,l):
                    if not first: act.wait_ge(s_tst[l],16*i)
                    return A.copy(B.row[:,:,0:16],B.ps[1][:,0:D].rearrange("p (t f) -> p t f",t=4))
                step(hgs,"pe:hg")
            gat(0,True)
            with act.Fori(1,GI) as i:
                gat(i,False)
            ended(act,GL,G_STEPS,GI)
            def terms(i):
                for g in range(2):
                    act.wait_ge(s_gat[g],256*(i+1))
                    A.copy(asx[:,:,bass.ds(i*32+g*16,16)],gs[:,g,:,16:20].rearrange("p c f -> p f c"))
                    A.copy(adx[:,:,bass.ds(i*32+g*16,16)],gs[:,g,:,20:24].rearrange("p c f -> p f c")).then_inc(s_acp,1)
            def both(i,gathers):
                for u in range(max(4,gathers)):
                    if u<4:
                        for B in YL:
                            need(act,B,Y_STEPS,i,f"pe:h{u}")
                            A.activation(B.hT[:,u%2,:],B.ps[u%2][:,:],ACT.Gelu,bias=lb1[:,u:u+1]).then_inc(B.act,1)
                    if u<gathers: terms(i*GPY+u)
            with act.Fori(0,GI-1) as i:
                both(i,GPY)
            both(GI-1,GN-(GI-1)*GPY)
            act.wait_ge(s_adm,1)
            A.activation(asx,asx,ACT.Exp).then_inc(s_exp,1)
            act.wait_ge(s_fl,2)
            over=act.value_load(flag_i[0:1,0:1],min_val=0,max_val=P)
            with act.If(over>0):
                with act.Fori(0,EC) as i:
                    act.wait_ge(s_od,i*O_STEPS+12)
                    A.activation(oex,oex,ACT.Exp).then_inc(s_oa,1)
            act.wait_ge(s_la,17)
            A.activation(lst[:,2,:],lst[:,1,:],ACT.Ln,scale=1.0/16,bias=eps[:,0:1]).then_inc(s_lc,1)
            act.wait_ge(s_lc,9)
            A.activation(lst[:,3,:],lst[:,2,:],ACT.Exp,scale=-0.5).then_inc(s_lb,1)
            act.wait_ge(s_th,2)
            A.activation(dd,dd,ACT.Tanh,scale=0.5).then_inc(s_tw,1)

        @block.vector
        def _(dve):
            V=nc.vector; n=[0]
            def lk(ins):
                n[0]+=1; ins.then_inc(s_v,1); dve.wait_ge(s_v,n[0])
            PS0=PS[0][:,:].rearrange("p (u e) -> p u e",u=4)
            V.memset(bkt_b[:,EC:EC+32],0.0)
            V.memset(sent,SENT).then_inc(s_sent,1)
            dve.wait_ge(s_ld,32); dve.wait_ge(s_const,1)
            V.tensor_copy(iota_b[:,:],iota_i[:,:])
            V.tensor_copy(rowp_f[:,:],rowp_i[:,:])
            lk(V.tensor_scalar(tmp_i[:,:],dst_i[:,:],127,None,ALU.bitwise_and))
            V.tensor_copy(bkt_f[:,:],tmp_i[:,:])
            lk(V.tensor_copy(bkt_b[:,0:EC],tmp_i[:,:]))
            lk(V.tensor_scalar(tmp_i[:,:],dst_i[:,:],7,15,ALU.logical_shift_right,ALU.logical_shift_left))
            lk(V.tensor_tensor(tmp_i[:,:],tmp_i[:,:],src_i[:,:],ALU.bitwise_or))
            lk(V.tensor_scalar(tmp_i[:,:],tmp_i[:,:],16384,None,ALU.bitwise_or))
            lk(V.tensor_copy(key_all,tmp_i[:,:]))
            def build(col,s):
                return V.tensor_tensor(oh[:,s,:,:], bkt_b[:,bass.ds(col,4)].unsqueeze(2).broadcast_to((P,4,P)), iota_b[:,:].unsqueeze(1).broadcast_to((P,4,P)),ALU.is_equal)
            build(0,0).then_inc(s_oh,1)
            def ranks(i):
                for g in range(2):
                    for q in range(4):
                        s=q%2
                        k=i*8+g*4+q
                        dve.wait_ge(s_post,k+1)
                        build(i*32+g*16+q*4+4,1-s).then_inc(s_oh,1)
                        dve.wait_ge(s_pre,k+1)
                        for u in range(4):
                            r=V.tensor_tensor_reduce(junk[:,u,:],oh[:,s,u,:],PS0[:,u,:],1.0,0.0,ALU.mult,ALU.add,rank16[:,g,4*q+u:4*q+u+1])
                        r.then_inc(s_rd,1)
                    j=2*i+g
                    dve.wait_ge(s_rd,4*j+4)
                    V.tensor_copy(rank_f[:,bass.ds(i*32+g*16,16)],rank16[:,g,:])
                    V.tensor_scalar(ovf16[:,g,:],rank16[:,g,:],float(EW),OOB,ALU.is_ge,ALU.mult)
                    V.scalar_tensor_tensor(out=idxf16[:,g,:],in0=bkt_f[:,bass.ds(i*32+g*16,16)],scalar=float(EW),in1=rank16[:,g,:],op0=ALU.mult,op1=ALU.add).then_inc(s_pair,1)
                    dve.wait_ge(s_pair,j+1)
                    V.tensor_tensor(idx_all[:,bass.ds(i*32+g*16,16)],idxf16[:,g,:],ovf16[:,g,:],ALU.add).then_inc(s_stage,1)
            with dve.Fori(0,EC//32) as i:
                ranks(i)
            lk(V.tensor_reduce(flagt[:,0:1],rank_f,AX.X,ALU.max))
            V.tensor_copy(flagt[:,1:2],flagt[:,0:1]).then_inc(s_rk,1)
            dve.wait_ge(s_rks,16); dve.wait_ge(s_post,EC//4+1)
            V.tensor_copy(rowbase[:,:],rowp_f[:,:]).then_inc(s_bn,1)
            dve.wait_ge(s_bn,1)
            for l in range(LANES):
                V.memset(L[l].x[:,0:1],0.0)
            V.memset(lnb[:,0:1],float(15*np.log(2.0))); V.memset(lnb[:,1:2],D*1e-5)
            dve.wait_ge(s_c,1); dve.wait_ge(s_w,16*16)
            lk(V.tensor_copy(ip[:,:],ip_i[:,:]))
            lk(V.tensor_scalar(pb_i[:,:],pb_i[:,:],4,None,ALU.logical_shift_right))
            V.tensor_copy(pb_f[:,:],pb_i[:,:])
            lk(V.tensor_copy(mrep[:,3,:],jb_i[:,:]))
            lk(V.tensor_scalar(mrep[:,3,:],mrep[:,3,:],pb_f[:,0:1],None,ALU.is_equal))
            for s in (slice(0,D),slice(D,P)):
                V.tensor_copy(i64[s,:],ident[0:D,0:D])
                V.tensor_tensor(mg1[s,0,:],mrep[:,0,:],mrep[:,3,:],ALU.mult)
                V.tensor_copy(mg1[s,1,:],mrep[:,1,:])
                V.tensor_copy(mg2[s,0,:],mrep[:,0,:]); V.tensor_copy(mg2[s,1,:],mrep[:,1,:])
                lk(V.tensor_tensor(ml[s,0,:],mrep[:,2,:],mrep[:,3,:],ALU.mult))
                V.tensor_tensor(ml[s,1,:],mrep[:,2,:],ml[s,0,:],ALU.subtract) if s.start==0 else V.tensor_copy(ml[s,1,:],ml[0:D,1,:])
                lk(V.tensor_copy(tst[:,0:1],ip[:,0:1]))
            for q,m in enumerate(["mr","mk","mw","ma"]):
                V.tensor_scalar(ws[:,q,:],raw[:,q,:],col(m),None,ALU.mult)
            V.tensor_scalar(vs[:,:],vraw[:,:],col("mv"),None,ALU.mult)
            V.tensor_scalar(cols[:,11:13],cols[:,0:2],0.5,None,ALU.mult)
            V.tensor_scalar(col("nk_a"),col("k_a"),-1.0,1.0,ALU.mult,ALU.add)
            lk(V.tensor_scalar(gsf[:,:,:],graw[:,:,:],col("mg"),None,ALU.mult))
            V.tensor_tensor(wx[:,:,:],raw[:,:,:],ws[:,:,:],ALU.subtract)
            V.tensor_tensor(vx[:,:],vraw[:,:],vs[:,:],ALU.subtract)
            lk(V.tensor_tensor(gx[:,:,:],graw[:,:,:],gsf[:,:,:],ALU.subtract))
            dve.wait_ge(s_t,2)
            bc=lambda r: rows[:,r,:].unsqueeze(1).broadcast_to((P,2,D))
            h0=tab[:,:,D:2*D]; xl=tab[:,:,0:D]
            lk(V.tensor_tensor(h0,L[0].ps[1][:,0:2*D].rearrange("p (v d) -> p v d",v=2),bc(0),ALU.add))
            def norm(dst,k):
                lk(V.tensor_reduce(tst[:,2:4],h0,AX.X,ALU.add))
                lk(V.tensor_scalar(tst[:,2:4],tst[:,2:4],1.0/D,None,ALU.mult))
                lk(V.tensor_tensor(dst,h0,tst[:,2:4].unsqueeze(2).broadcast_to((P,2,D)),ALU.subtract))
                lk(V.tensor_tensor(tm[:,:,:],dst,dst,ALU.mult))
                lk(V.tensor_reduce(tst[:,2:4],tm[:,:,:],AX.X,ALU.add))
                V.tensor_scalar(tst[:,2:4],tst[:,2:4],1.0/D,EPS,ALU.mult,ALU.add).then_inc(s_tv,1)
                dve.wait_ge(s_ta,3+2*k)
                lk(V.tensor_tensor(dst,dst,tst[:,0:2].unsqueeze(2).broadcast_to((P,2,D)),ALU.mult))
            norm(h0,0)
            lk(V.tensor_tensor(h0,h0,bc(1),ALU.mult))
            lk(V.tensor_tensor(h0,h0,bc(2),ALU.add))
            norm(xl,1)
            V.tensor_copy(tst[:,0:1],ip[:,0:1]).then_inc(L[0].dve,1)
            V.tensor_copy(tst[:,1:2],ip[:,0:1]).then_inc(L[1].dve,1)
            V.tensor_copy(tst[:,2:3],ip[:,0:1]).then_inc(s_tt,1)
            SORT=sort_steps(SW)
            def sort_step(k):
                st=SORT[k]; a=k%2
                x,y=K[a],K[1-a]
                for kind,s,nb,w in st:
                    if kind=="copy":
                        last=V.tensor_copy(y[:,s:s+w],x[:,s:s+w])
                    elif kind in("flip","half"):
                        h=w//2
                        X=x[:,s:s+nb*w].rearrange("p (b w) -> p b w",w=w); Y=y[:,s:s+nb*w].rearrange("p (b w) -> p b w",w=w)
                        hi=X[:,:,h:w]; yh=Y[:,:,h:w]
                        if kind=="flip":
                            hi=X[:,:,h:w][:,:,::-1]; yh=Y[:,:,h:w][:,:,::-1]
                        V.tensor_tensor(Y[:,:,0:h],X[:,:,0:h],hi,ALU.min)
                        last=V.tensor_tensor(yh,X[:,:,0:h],hi,ALU.max)
                    elif kind=="rflip":
                        h=nb
                        lo=x[:,s+h-w:s+h]; hi=x[:,s+h:s+h+w][:,::-1]
                        V.tensor_tensor(y[:,s+h-w:s+h],lo,hi,ALU.min)
                        last=V.tensor_tensor(y[:,s+h:s+h+w][:,::-1],lo,hi,ALU.max)
                    else:
                        d=nb
                        lo=x[:,s:s+w]; hi=x[:,s+d:s+d+w]
                        V.tensor_tensor(y[:,s:s+w],lo,hi,ALU.min)
                        last=V.tensor_tensor(y[:,s+d:s+d+w],lo,hi,ALU.max)
                lk(last)
            wait=mk(dve,"dve")
            r4=lambda t,k: t.unsqueeze(1).broadcast_to((P,4)+tuple(t.shape[1:]))
            s4=lambda t: t.unsqueeze(2).broadcast_to((P,4,D))
            calls=[0]
            def it(i,sorting=False):
                def step(fn,*need):
                    for l in range(LANES):
                        wait(l,i,*need)
                        fn(L[l],l).then_inc(L[l].dve,1)
                    if sorting:
                        calls[0]+=1
                        if calls[0]%2==0 and calls[0]//2<=len(SORT): sort_step(calls[0]//2-1)
                def oneh(B,l):
                    dve.wait_ge(B.ld,16*i+16)
                    V.tensor_scalar(B.oneh[:,0,:],B.tk[:,:],ip[:,0:1],None,ALU.is_equal)
                    return V.tensor_scalar(B.oneh[:,1,:],B.tk[:,:],ip[:,1:2],None,ALU.is_equal)
                step(oneh)
                step(lambda B,l:V.tensor_scalar(B.sg[:,:,:],B.sg[:,:,:],0.5,0.5,ALU.mult,ALU.add),"act:sgt")
                step(lambda B,l:V.tensor_scalar(B.w[:,:],B.w[:,:],DECAY/2,DECAY/2,ALU.mult,ALU.add),"act:tw")
                step(lambda B,l:V.tensor_tensor_scan(B.cs[:,:],flag[:,:],B.w[:,:],0.0,ALU.mult,ALU.add),"dve:w")
                step(lambda B,l:V.tensor_tensor(B.cm[:,:],B.cs[:,:],B.w[:,:],ALU.subtract),"dve:cs")
                step(lambda B,l:V.tensor_scalar(B.a[:,:],B.a[:,:],0.5,0.5,ALU.mult,ALU.add),"act:ta")
                step(lambda B,l:V.tensor_scalar(B.kq[:,:],B.ps[0][:,T:2*T],col("k_k"),None,ALU.mult),"act:sq")
                step(lambda B,l:V.tensor_scalar(B.b0[:,:],B.ps[2][:,0:T],1e-24,None,ALU.max),"pe:ss")
                step(lambda B,l:V.tensor_tensor(B.kq[:,:],B.kq[:,:],B.rn[:,:],ALU.mult),"act:rn","dve:kq")
                step(lambda B,l:V.scalar_tensor_tensor(out=B.AR[:,:,0,:],in0=c4(B.kq),scalar=-1.0,in1=c4(B.e2),op0=ALU.mult,op1=ALU.mult),"dve:kn","act:e2")
                step(lambda B,l:V.tensor_tensor(B.AR[:,:,1,:],c4(B.ps[0][:,0:T]),c4(B.e1),ALU.mult),"act:e1")
                step(lambda B,l:V.tensor_tensor(B.b0[:,:],B.kq[:,:],B.a[:,:],ALU.mult),"act:lnk","dve:a")
                step(lambda B,l:V.tensor_tensor(B.B[:,:],B.b0[:,:],B.e3[:,:],ALU.mult),"act:e3","dve:b0")
                step(lambda B,l:V.tensor_scalar(B.kp[:,:],B.a[:,:],col("k_a"),col("nk_a"),ALU.mult,ALU.add))
                step(lambda B,l:V.tensor_tensor(B.kp[:,:],B.ps[0][:,T:2*T],B.kp[:,:],ALU.mult),"dve:t1")
                step(lambda B,l:V.tensor_tensor(B.K[:,:],B.kp[:,:],B.e3[:,:],ALU.mult),"dve:kp")
                step(lambda B,l:V.tensor_tensor(B.rk[:,:],B.ps[0][:,0:T],B.kp[:,:],ALU.mult))
                v3=lambda t: t.rearrange("p (c a t) -> p c a t",a=2,c=4)
                step(lambda B,l:V.tensor_tensor(B.g1[:,:,:,:],v3(B.ps[0][:,:]),r4(mg1[:,:,:],0),ALU.mult),"pe:G1")
                step(lambda B,l:V.tensor_tensor(B.g2[:,:,:,:],v3(B.ps[2][:,:]),r4(mg2[:,:,:],0),ALU.mult),"pe:G2")
                step(lambda B,l:V.tensor_tensor(B.lo[:,0,:,:],c4(B.ps[1][:,0:T]),r4(ml[:,0,:],0),ALU.mult),"pe:L")
                step(lambda B,l:V.tensor_tensor(B.lo[:,1,:,:],c4(B.ps[1][:,0:T]),r4(ml[:,1,:],0),ALU.mult))
                step(lambda B,l:V.tensor_tensor(B.dta[:,:,:],B.g1[:,:,0,:],r4(i64[:,:],0),ALU.add),"dve:g1")
                step(lambda B,l:V.tensor_tensor(B.dtb[:,:,:],c4(B.ps[0][:,0:T]),B.dta[:,:,:],ALU.add),"pe:x2","dve:d1")
                step(lambda B,l:V.tensor_tensor(B.dta[:,:,:],c4(B.ps[0][:,T:2*T]),B.dtb[:,:,:],ALU.add),"pe:x4","dve:d2")
                step(lambda B,l:V.tensor_tensor(B.dtb[:,:,:],c4(B.ps[1][:,T:2*T]),B.dta[:,:,:],ALU.add),"pe:x8","dve:d4")
                step(lambda B,l:V.tensor_tensor(B.Z1[:,:,:,:],v3(B.ps[1][:,:]),B.Z0[:,:,:,:],ALU.add),"pe:Z1")
                step(lambda B,l:V.tensor_tensor(B.Wy[:,:,:,:],v3(B.ps[3][:,:]),B.Z1[:,:,:,:],ALU.add),"pe:W","dve:Z1")
                for c in range(1,4):
                    step(lambda B,l:V.tensor_tensor(B.U[:,c,:],B.ps[2][:,c*D:(c+1)*D],B.Wy[:,c,0,:],ALU.add),f"pe:U{c}","dve:W")
                step(lambda B,l:V.tensor_reduce(B.st[:,:,0],B.O[:,:,:],AX.X,ALU.add),"act:Os")
                def oc(B,l):
                    return V.scalar_tensor_tensor(out=B.oc[:,:,:],in0=s4(B.st[:,:,0]),scalar=-1.0/D,in1=B.O[:,:,:],op0=ALU.mult,op1=ALU.add)
                step(oc,"dve:mu")
                def var(B,l):
                    return V.tensor_reduce(B.st[:,:,1],B.osq[:,:,:],AX.X,ALU.add)
                step(var,"act:osq")
                step(lambda B,l:V.tensor_tensor(B.oc[:,:,:],B.oc[:,:,:],s4(B.st[:,:,3]),ALU.mult),"act:rstd")
                step(lambda B,l:V.tensor_tensor(B.oc[:,:,:],B.oc[:,:,:],r4(rows[:,3,:],0),ALU.mult),"dve:on")
                step(lambda B,l:V.tensor_tensor(B.oc[:,:,:],B.oc[:,:,:],r4(rows[:,4,:],0),ALU.add),"dve:gw")
                step(lambda B,l:V.tensor_tensor(B.O[:,:,:],B.V[:,:,:],s4(B.bon[:,:]),ALU.mult),"act:bons")
                step(lambda B,l:V.tensor_tensor(B.oc[:,:,:],B.oc[:,:,:],B.O[:,:,:],ALU.add),"dve:gb","dve:bv")
                step(lambda B,l:V.tensor_tensor(B.oc[:,:,:],B.oc[:,:,:],B.gt[:,:,:],ALU.mult),"dve:ob")
                step(lambda B,l:V.tensor_tensor(H[:,bass.ds((i*LANES+l)*4,4),:].rearrange("p (h t) d -> p h t d",t=2),B.ps[0][:,T:2*T].rearrange("p (t h d) -> p h t d",t=2,h=2),B.h0[:,:,:].rearrange("p (h t) d -> p h t d",t=2),ALU.add),"pe:wo","act:h0s")
            with dve.Fori(0,ITERS-SORT_ITERS) as i:
                it(i)
            lk(V.tensor_scalar(K[0][:,0:P],iota_i[:,:],float(KS),None,ALU.mult))
            dve.wait_ge(s_bk,16)
            for i in range(ITERS-SORT_ITERS,ITERS):
                it(i,True)
            assert calls[0]//2>=len(SORT)
            for l in range(LANES):
                dve.wait_ge(L[l].pe,ITERS*len(PE_STEPS)); dve.wait_ge(L[l].act,ITERS*len(ACT_STEPS)); dve.wait_ge(L[l].dve,ITERS*len(DVE_STEPS)+1)
            key,t=K[len(sort_steps(SW))%2],heads
            ki=neg[:,0:SW].bitcast(I32); ti=gidx[:,:]
            lk(V.tensor_copy(ki[:,:],key[:,:]))
            lk(V.tensor_scalar(ti[:,:],ki[:,:],14,1,ALU.logical_shift_right,ALU.bitwise_and))
            lk(V.tensor_copy(cont[:,:],ti[:,:]))
            lk(V.tensor_scalar(t[:,:],key[:,:],SENT,None,ALU.is_lt))
            V.tensor_reduce(nreal[:,:],t[:,:],AX.X,ALU.add)
            lk(V.scalar_tensor_tensor(out=t[:,:],in0=cont[:,:],scalar=0.5,in1=t[:,:],op0=ALU.is_lt,op1=ALU.mult))
            dve.wait_ge(s_ci,1)
            lk(V.tensor_tensor(t[:,:],t[:,:],col_i[:,:],ALU.mult))
            for r in range(P//8):
                lk(V.max(v8[:,8*r:8*r+8],t[:,:]))
                lk(V.match_replace(t[:,:],v8[:,8*r:8*r+8],t[:,:],0.0))
            V.tensor_scalar(endf[:,0:P-1],v8[:,1:P],-1.0,4095.0,ALU.mult,ALU.add)
            lk(V.tensor_scalar(endf[:,P-1:P],nreal[:,:],-1.0,None,ALU.add))
            lk(V.tensor_scalar(rowbase[:,:],rowp_f[:,:],float(SW),None,ALU.mult))
            V.tensor_scalar(end_i[:,:],endf[:,:],rowbase[:,0:1],None,ALU.add).then_inc(s_ei,1)
            lk(V.tensor_scalar(ti[:,:],ki[:,:],15,7,ALU.logical_shift_right,ALU.logical_shift_left))
            lk(V.tensor_copy(t[:,:],ti[:,:]))
            lk(V.tensor_scalar(t[:,:],t[:,:],rowp_f[:,0:1],None,ALU.add))
            lk(V.tensor_scalar(ki[:,:],ki[:,:],16383,None,ALU.bitwise_and))
            lk(V.scalar_tensor_tensor(out=t[:,:],in0=cont[:,:],scalar=0.5,in1=t[:,:],op0=ALU.is_lt,op1=ALU.mult))
            lk(V.tensor_tensor(t[:,:],t[:,:],ki[:,:],ALU.add))
            V.memset(neg[:,SW:SW+1],-BIG)
            V.tensor_scalar(gidx[:,:],t[:,:],float(M-1),None,ALU.min).then_inc(s_gi,1)
            dve.wait_ge(s_gi,1)
            V.tensor_scalar(neg[:,0:SW],cont[:,:],-1.0,BIG,ALU.add,ALU.mult)
            lk(V.tensor_scalar(t[:,:],cont[:,:],0.5,None,ALU.is_lt))
            lk(V.memset(eps[:,:],EPS))
            dve.wait_ge(s_mc,1)
            lk(V.tensor_copy(iot[:,:],iot_i[:,:]))
            nl=[0]; nb=[0]
            def norm(src,dst):
                for c in range(2):
                    h=slice(c*D,(c+1)*D); row=lambda k: lst[:,k,h].unsqueeze(2).broadcast_to((P,D,D))
                    lk(V.tensor_reduce(lst[:,0,h],src[:,h,:],AX.X,ALU.add))
                    V.scalar_tensor_tensor(out=dst[:,h,:],in0=row(0),scalar=-1.0/D,in1=src[:,h,:],op0=ALU.mult,op1=ALU.add).then_inc(s_la,1)
                    nl[0]+=1; nb[0]+=1; dve.wait_ge(s_la,nl[0]); dve.wait_ge(s_lb,nb[0])
                    V.tensor_reduce(lst[:,1,h],sq[:,h,:],AX.X,ALU.add).then_inc(s_la,1)
                    nl[0]+=1; nb[0]+=1; dve.wait_ge(s_lb,nb[0])
                    lk(V.tensor_tensor(dst[:,h,:],dst[:,h,:],row(3),ALU.mult))
            norm(H[:,:,:],xn)
            norm(xn,xn)
            for B in FL:
                V.memset(B.mf[:,:,:],0.0)
                last=V.memset(B.xT[D:D+1],1.0)
            last.then_inc(s_one,1)
            dve.wait_ge(s_one,1)
            dve.wait_ge(s_fw,16*6)
            b4=lambda t: t.unsqueeze(1).broadcast_to((P,4)+tuple(t.shape[1:]))
            with dve.Fori(0,GI) as i:
                def step(fn,*names):
                    for l,B in enumerate(FL):
                        need(dve,B,F_STEPS,i,*names)
                        fn(B,l).then_inc(B.dve,1)
                step(lambda B,l:V.tensor_tensor(B.xs,xn[:,bass.ds((i*2+l)*4,4),:],b4(fgam[:,0,:]),ALU.mult))
                step(lambda B,l:V.tensor_tensor(B.xs,B.xs,b4(fgam[:,1,:]),ALU.add),"dve:xg")
                def mx(B,l):
                    V.tensor_copy(B.dm[:,0:1],B.mf[:,0,0:1])
                    for t in range(4): r=V.max(B.mx[:,t,:],B.lg[:,t,:])
                    return r
                step(mx,"act:lgs")
                def mi(B,l):
                    V.tensor_copy(B.dm[:,0:1],B.mx[:,0,0:1])
                    for t in range(4): r=V.max_index(B.mi[:,t,:],B.mx[:,t,:],B.lg[:,t,:])
                    return r
                step(mi,"dve:mx")
                step(lambda B,l:V.tensor_copy(B.mf,B.mi[:,:,0:2]),"dve:mi")
                step(lambda B,l:V.tensor_tensor(B.dd,B.mx[:,:,0],B.mx[:,:,1],ALU.subtract))
                step(lambda B,l:V.tensor_scalar(B.w12[:,:,0],B.dd,0.5,0.5,ALU.mult,ALU.add),"act:th")
                step(lambda B,l:V.tensor_scalar(B.w12[:,:,1],B.dd,-0.5,0.5,ALU.mult,ALU.add))
                i8=iot[:,:].unsqueeze(1).broadcast_to((P,4,8)); q8=lambda B,k: B.q[:,k,:].rearrange("p (a b) -> p a b",a=4)
                e8=lambda t: t.unsqueeze(2).broadcast_to((P,4,8))
                for k in range(2):
                    step(lambda B,l:V.tensor_tensor(q8(B,k),i8,e8(B.mf[:,:,k]),ALU.is_equal),"dve:mf")
                for k in range(2):
                    step(lambda B,l:V.tensor_tensor(q8(B,k),q8(B,k),e8(B.w12[:,:,k]),ALU.mult),"dve:q1","dve:w2")
                step(lambda B,l:V.tensor_tensor(B.wf,q8(B,0),q8(B,1),ALU.add),"dve:q1w")
                for p in range(4):
                    step(lambda B,l:V.tensor_tensor(B.tmp,B.ps[2][:,:].rearrange("p (t e d) -> p t e d",t=4,e=2),B.wf[:,:,2*p:2*p+2].unsqueeze(3).broadcast_to((P,4,2,D)),ALU.mult),f"pe:y{2*p+1}",*(["dve:wf"] if p==0 else [f"dve:yb{p-1}"]))
                    if p==0:
                        step(lambda B,l:V.tensor_copy(B.acc,B.tmp[:,:,0,:]),f"dve:ym{p}")
                    else:
                        step(lambda B,l:V.tensor_tensor(B.acc,B.acc,B.tmp[:,:,0,:],ALU.add),f"dve:ym{p}")
                    step(lambda B,l:V.tensor_tensor(B.acc,B.acc,B.tmp[:,:,1,:],ALU.add),f"dve:ya{p}")
                step(lambda B,l:V.tensor_tensor(B.acc,B.acc,four(B.ps[3][:,0:256]),ALU.add),"pe:bias","dve:yb3")
                def hh(B,l):
                    v=H[:,bass.ds((i*2+l)*4,4),:]
                    return V.tensor_tensor(v,v,B.acc,ALU.add)
                step(hh,"dve:ab")
            ended(dve,FL,F_STEPS,GI)
            norm(H[:,:,:],xn)
            V.memset(eps[:,:],EPS)
            lk(V.tensor_scalar(mk_i[:,1:2],mk_i[:,0:1],63,3,ALU.bitwise_and,ALU.logical_shift_right))
            lk(V.tensor_scalar(mk_i[:,0:1],mk_i[:,0:1],6,None,ALU.logical_shift_right))
            lk(V.tensor_copy(mkf[:,:],mk_i[:,:]))
            V.tensor_scalar(hmask,iot[:,:],mkf[:,1:2],None,ALU.is_equal)
            V.tensor_scalar(vmask,iot[:,0:2],mkf[:,0:1],None,ALU.is_equal)
            for B in AL:
                V.memset(B.xT[D:D+1],1.0); V.memset(B.oT[D:D+1],1.0)
                V.memset(B.Q[0:D,D:P],0.0); V.memset(B.Q[D:P,0:D],0.0).then_inc(B.dve,1)
            for B in AL: dve.wait_ge(B.dve,1)
            dve.wait_ge(s_w2,16*8)
            h8=lambda t: t.unsqueeze(2).broadcast_to((P,8,D))
            sc=lambda B: B.ps[1][:,:].rearrange("p (h j) -> p h j",h=8)
            with dve.Fori(0,AI) as i:
                def step(fn,*names):
                    for l,B in enumerate(AL):
                        need(dve,B,A_STEPS,i,*names)
                        fn(B,l).then_inc(B.dve,1)
                step(lambda B,l:V.tensor_tensor(B.K,B.ps[0][:,P+D:2*P].unsqueeze(1).broadcast_to((P,8,D)),h8(hmask),ALU.mult),"act:q")
                def vb(B,l):
                    v=lambda t: t.rearrange("p (g e d) -> p g e d",g=8,e=2)
                    return V.tensor_tensor(v(B.V.rearrange("p w f -> p (w f)")),v(B.ps[0][:,2*P:3*P]),vmask.unsqueeze(1).unsqueeze(3).broadcast_to((P,8,2,8)),ALU.mult)
                step(vb,"pe:qkv")
                step(lambda B,l:V.tensor_reduce(B.mx,sc(B),AX.X,ALU.max),"pe:sc")
                step(lambda B,l:V.tensor_tensor(B.E,sc(B),h8(B.mx),ALU.subtract),"dve:mx")
                step(lambda B,l:V.tensor_reduce(B.rs,B.E,AX.X,ALU.add),"act:ex")
                step(lambda B,l:V.reciprocal(B.rs,B.rs),"dve:sm")
                step(lambda B,l:V.tensor_tensor(B.o.rearrange("p (h d) -> p h d",h=8),B.ps[0][:,384:448].rearrange("p (h d) -> p h d",h=8),B.rs.unsqueeze(2).broadcast_to((P,8,8)),ALU.mult),"pe:pv","dve:rc")
                def hh(B,l):
                    v=H[:,bass.ds(i*4+l,1),:]
                    return V.tensor_tensor(v,v,B.ps[0][:,448:512].unsqueeze(1),ALU.add)
                step(hh,"pe:pj")
            ended(dve,AL,A_STEPS,AI)
            norm(H[:,:,:],xn)
            with dve.Fori(0,GI) as i:
                def step(fn,*names):
                    for l,B in enumerate(GL):
                        need(dve,B,G_STEPS,i,*names)
                        fn(B,l).then_inc(B.dve,1)
                for k,(m,r_) in enumerate((("hgs","ms"),("hgs","md"))):
                    step(lambda B,l:V.tensor_tensor(B.tm,B.row[:,:,0:16],b4(gatt[:,k,:]),ALU.mult),"act:hgs",*(["dve:rs"] if k else []))
                    step(lambda B,l:V.tensor_reduce(B.row[:,:,16+4*k:20+4*k],B.tm.rearrange("p t (g e) -> p t g e",g=4),AX.X,ALU.add),f"dve:{r_}")
            ended(dve,GL,G_STEPS,GI)
            def bias1(i,first):
                for q in range(2):
                    for l,B in enumerate(YL):
                        if not first: dve.wait_ge(s_yst[q][l],16*i)
                        need(dve,B,Y_STEPS,i,f"pe:y{2*q+1}")
                        v=lambda t: t.rearrange("p (t f) -> p t f",t=4)
                        V.tensor_tensor(v(B.ys[:,q,:]),v(B.ps[2+q][:,:]),b4(lb2[:,2*q:2*q+2,:].rearrange("p a b -> p (a b)")),ALU.add).then_inc(B.dve,1)
            bias1(0,True)
            with dve.Fori(1,GI) as i:
                bias1(i,False)
            dve.wait_ge(s_acp,SW//16)
            for f in range(4):
                last=V.tensor_tensor(adx[:,f,:],adx[:,f,:],t[:,:],ALU.mult)
            lk(last)
            for f in range(4):
                last=V.tensor_tensor_scan(adx[:,f,:],cont[:,:],adx[:,f,:],0.0,ALU.mult,ALU.add)
            lk(last)
            lk(V.tensor_tensor(asx[:,:,:],asx[:,:,:],adx[:,:,:],ALU.add))
            lk(V.scalar_tensor_tensor(out=asx[:,:,:],in0=asx[:,:,:],scalar=0.2,in1=asx[:,:,:],op0=ALU.mult,op1=ALU.max))
            for f in range(4):
                last=V.tensor_tensor_scan(adx[:,f,:],neg[:,0:SW],asx[:,f,:],-BIG,ALU.add,ALU.max)
            lk(last)
            for f in range(4):
                last=V.tensor_tensor_scan(adx[:,f,:][:,::-1],neg[:,1:SW+1][:,::-1],adx[:,f,:][:,::-1],-BIG,ALU.add,ALU.max)
            lk(last)
            V.tensor_tensor(asx[:,:,:],asx[:,:,:],adx[:,:,:],ALU.subtract).then_inc(s_adm,1)
            dve.wait_ge(s_exp,1)
            for c in range(NCH):
                b=c%2; c0=c*CH
                dve.wait_ge(s_rld[b],16*(c//2+1))
                R=rch[:,b,:,:]; ev=asx[:,:,c0:c0+CH].rearrange("p f c -> p c f")
                h4=R[:,:,0:16].rearrange("p c (g e) -> p c g e",g=4)
                V.tensor_copy(R[:,:,20:24],adx[:,:,c0:c0+CH].rearrange("p f c -> p c f"))
                V.tensor_copy(R[:,:,16:20],ev)
                lk(V.tensor_tensor(h4,h4,ev.unsqueeze(3).broadcast_to((P,CH,4,4)),ALU.mult))
                for f in range(20):
                    last=V.tensor_tensor_scan(R[:,:,f],cont[:,c0:c0+CH],R[:,:,f],0.0 if c==0 else carry[:,1-b,f:f+1],ALU.mult,ALU.add)
                lk(last)
                V.tensor_copy(carry[:,b,:],R[:,CH-1,:]).then_inc(s_sum,1)
                dve.wait_ge(s_sum,c+1)
            dve.wait_ge(s_eg,16*P)
            V.tensor_scalar(flagt[:,1:2],flagt[:,0:1],float(EW),None,ALU.is_ge).then_inc(s_fl,1)
            dve.wait_ge(s_fp,1)
            V.tensor_copy(flag_i[0:1,:],PS[7][0:1,0:1]).then_inc(s_fl,1)
            dve.wait_ge(s_fl,2)
            over=dve.value_load(flag_i[0:1,0:1],min_val=0,max_val=P)
            with dve.If(over>0):
                dve.wait_ge(s_ol,48)
                V.tensor_scalar(o_rank,o_rank,float(EW),float(M),ALU.is_lt,ALU.mult).then_inc(s_of,1)
                V.tensor_copy(o_key,o_dst).then_inc(s_of,1)
                dve.wait_ge(s_of,2)
                V.tensor_tensor(o_key,o_key,o_rank,ALU.add).then_inc(s_of,1)
                dve.wait_ge(s_of,3)
                V.tensor_copy(o_keyi,o_key).then_inc(s_of,1)
                dve.wait_ge(s_of,4)
                with dve.Fori(0,EC) as i:
                    k=[0]
                    def st(ins):
                        k[0]+=1; ins.then_inc(s_od,1); dve.wait_ge(s_od,i*O_STEPS+k[0])
                    at=bass.ds(i,1); h4=lambda t: t.rearrange("p (g e) -> p g e",g=4); g4=lambda t: t.unsqueeze(2).broadcast_to((P,4,4))
                    erow,rowd,state=orow[:,0,:],orow[:,1,:],orow[:,2,:]
                    V.tensor_copy(oix[:,0:1],o_src[:,at]); V.tensor_copy(oix[:,1:2],o_dst[:,at]); V.tensor_copy(okey,o_key[:,at])
                    st(V.tensor_copy(oix[:,2:3],o_keyi[:,at]))
                    st(V.tensor_tensor(odg[:,0,:],ident[:,:],okey.broadcast_to((P,P)),ALU.mult))
                    for g in range(3): dve.wait_ge(s_og[g],16*i+16)
                    st(V.tensor_tensor(osc,erow[:,16:20],rowd[:,20:24],ALU.add))
                    st(V.scalar_tensor_tensor(out=osc,in0=osc,scalar=0.2,in1=osc,op0=ALU.mult,op1=ALU.max))
                    st(V.tensor_tensor(odg[:,1:5,:],ident[:,:].unsqueeze(1).broadcast_to((P,4,P)),osc.unsqueeze(2).broadcast_to((P,4,P)),ALU.mult))
                    dve.wait_ge(s_op,2*i+1)
                    st(V.tensor_tensor(osel,PS[6][:,0:P],okey.broadcast_to((P,P)),ALU.is_equal))
                    st(V.tensor_scalar(oneg,osel,-1.0,BIG,ALU.add,ALU.mult))
                    st(V.tensor_tensor(otm,PS[7][:,:].rearrange("p (g e) -> p g e",g=4),oneg.unsqueeze(1).broadcast_to((P,4,P)),ALU.add))
                    st(V.tensor_reduce(onm,otm,AX.X,ALU.max))
                    st(V.tensor_tensor(onm,onm,state[:,20:24],ALU.max))
                    st(V.tensor_tensor(oex[:,0,:],osc,onm,ALU.subtract))
                    st(V.tensor_tensor(oex[:,1,:],state[:,20:24],onm,ALU.subtract))
                    dve.wait_ge(s_oa,i+1)
                    st(V.tensor_tensor(h4(owv[:,0:16]),h4(erow[:,0:16]),g4(oex[:,0,:]),ALU.mult))
                    st(V.tensor_copy(owv[:,16:20],oex[:,0,:]))
                    V.tensor_tensor(h4(ost[:,0:16]),h4(state[:,0:16]),g4(oex[:,1,:]),ALU.mult)
                    V.tensor_copy(ost[:,20:24],onm)
                    st(V.tensor_tensor(ost[:,16:20],state[:,16:20],oex[:,1,:],ALU.mult))
                    dve.wait_ge(s_op,2*i+2)
                    st(V.tensor_tensor(ost[:,0:20],ost[:,0:20],PS[6][:,P:P+20],ALU.add))
                    assert k[0]==O_STEPS
                    dve.wait_ge(s_osc,16*i+16)
                dve.wait_ge(s_orl,16)
            lk(V.tensor_scalar(endd[:,:,:],ends[:,:,16:20],1e-16,None,ALU.add))
            lk(V.reciprocal(endd[:,:,:],endd[:,:,:]))
            dve.wait_ge(s_sst[0],16*(NCH//2)); dve.wait_ge(s_fin,16)
            lk(V.tensor_tensor(agg.rearrange("p n (g e) -> p n g e",g=4),ends[:,:,0:16].rearrange("p n (g e) -> p n g e",g=4),
                endd[:,:,:].unsqueeze(3).broadcast_to((P,P,4,4)),ALU.mult))
            r16=lambda k: fin[:,k,:].unsqueeze(1).broadcast_to((P,NT,16)); c16=lambda k: lst[:,k,:].unsqueeze(2).broadcast_to((P,NT,16))
            lk(V.tensor_tensor(agg,agg,r16(0),ALU.add))
            lk(V.tensor_reduce(lst[:,0,:],agg,AX.X,ALU.add))
            lk(V.scalar_tensor_tensor(out=agg,in0=c16(0),scalar=-1.0/16,in1=agg,op0=ALU.mult,op1=ALU.add))
            lk(V.tensor_tensor(asq,agg,agg,ALU.mult))
            V.tensor_reduce(lst[:,1,:],asq,AX.X,ALU.add).then_inc(s_la,1)
            V.memset(sc8[:,:,4:8],-BIG).then_inc(s_th,1)
            dve.wait_ge(s_lb,17); dve.wait_ge(s_th,1)
            lk(V.tensor_tensor(agg,agg,c16(3),ALU.mult))
            lk(V.tensor_tensor(agg,agg,r16(1),ALU.mult))
            lk(V.tensor_tensor(agg,agg,r16(2),ALU.add))
            lk(V.tensor_reduce(sc8[:,:,0:4],agg.rearrange("p n (g e) -> p n e g",g=4),AX.X,ALU.add))
            lk(V.tensor_scalar(sc8[:,:,0:4],sc8[:,:,0:4],0.25,None,ALU.mult))
            for t in range(NT): last=V.max(m8[:,t,:],sc8[:,t,:])
            lk(last)
            for t in range(NT): last=V.max_index(mi8[:,t,:],m8[:,t,:],sc8[:,t,:])
            lk(last)
            lk(V.tensor_copy(mf2,mi8[:,:,0:2]))
            V.tensor_tensor(dd,m8[:,:,0],m8[:,:,1],ALU.subtract).then_inc(s_th,1)
            dve.wait_ge(s_tw,1)
            V.tensor_scalar(w12[:,:,0],dd,0.5,0.5,ALU.mult,ALU.add)
            lk(V.tensor_scalar(w12[:,:,1],dd,-0.5,0.5,ALU.mult,ALU.add))
            e4=lambda t: t.unsqueeze(2).broadcast_to((P,NT,4))
            for k in range(2): last=V.tensor_tensor(q4[:,k],iot[:,0:4].unsqueeze(1).broadcast_to((P,NT,4)),e4(mf2[:,:,k]),ALU.is_equal)
            lk(last)
            for k in range(2): last=V.tensor_tensor(q4[:,k],q4[:,k],e4(w12[:,:,k]),ALU.mult)
            lk(last)
            lk(V.tensor_tensor(wf4,q4[:,0],q4[:,1],ALU.add))
            ey=lambda t: t.rearrange("p n (e d) -> p n e d",e=4)
            with dve.Fori(0,NT//16) as i:
                for b in range(2):
                    k=2*i+b
                    dve.wait_ge(s_yl[b],16*i+16)
                    V.tensor_tensor(ey(yt),ey(yb[b]),wf4[:,bass.ds(k*8,8),:].unsqueeze(3).broadcast_to((P,8,4,D)),ALU.mult).then_inc(s_yu,1)
                    dve.wait_ge(s_yu,k+1)
                    V.tensor_tensor(yt[:,:,0:2*D],yt[:,:,0:2*D],yt[:,:,2*D:4*D],ALU.add).then_inc(s_ya,1)
                    dve.wait_ge(s_ya,3*k+1)
                    V.tensor_tensor(yt[:,:,0:D],yt[:,:,0:D],yt[:,:,D:2*D],ALU.add).then_inc(s_ya,1)
                    dve.wait_ge(s_ya,3*k+2)
                    v=H[:,bass.ds(k*8,8),:]
                    V.tensor_tensor(v,v,yt[:,:,0:D],ALU.add).then_inc(s_ya,1)
                    dve.wait_ge(s_ya,3*k+3)
            V.tensor_copy(rowbase[:,:],rowp_f[:,:]).then_inc(s_fn,1)

_NAMES="x embT w1T tb1 w2T rows proj wv ag lora bg wo cols gam wr w1 b1 w2 b2 qkv proj1 wg att lw1 lb1 lw2 lb2 fin edges".split()
def kernel(**q):
    import numpy as _np
    import concourse.bacc as _bacc
    from concourse import mybir as _mybir
    from concourse.bass_utils import run_bass_kernel_spmd as _run
    a={k:_np.asarray(v) for k,v in q.items()}
    two=lambda w: _np.concatenate([w,w],0)
    c=lambda w: w.reshape(-1,1)
    rep=lambda v: _np.broadcast_to(v,(128,)+v.shape)
    aug=lambda w,b: _np.concatenate([w,b[None]],0)
    part=lambda p: {n[len(p):]:v for n,v in a.items() if n.startswith(p)}
    tok,g,f,t,m=part('L0_tok_'),part('L0_attn_'),part('L0_ffn_'),part('L1_attn_'),part('L1_ffn_')
    ins=dict(x=a['x'],embT=tok['emb_table'].T,w1T=tok['W1'][:,:64].T,tb1=c(tok['b1']),w2T=tok['W2'].T,
        rows=rep(_np.stack([tok['b2'],tok['gamma'],tok['beta'],g['gn_w'],g['gn_b']])),
        proj=_np.stack([g['W_r'],g['W_k'],g['A_w'],g['A_a']],1),wv=two(g['W_v']),ag=g['A_g'],
        lora=_np.stack([g['B_w'],g['B_a']],1),bg=g['B_g'],wo=g['W_o'],
        cols=_np.concatenate([two(c(g[n])) for n in ('b_w','b_a','k_k','k_a','r_k')]+[two(c(g['x_mix'][j])) for j in (0,1,2,3,4,5)],1),
        gam=rep(_np.stack([f['gamma'],f['beta']])),wr=aug(f['Wr'],f['br']),w1=f['W1'].transpose(1,0,2),b1=f['b1'].T,w2=f['W2'].transpose(1,0,2),b2=f['b2'],
        qkv=aug(t['qkv_w'],t['qkv_b']),proj1=aug(t['proj_w'],t['proj_b']),wg=m['W_gat'],att=rep(_np.stack([m['att_src'].reshape(16),m['att_dst'].reshape(16)])),
        lw1=m['W1'].transpose(1,0,2),lb1=m['b1'].T,lw2=m['W2'].transpose(1,0,2),lb2=rep(m['b2']),
        fin=rep(_np.stack([m['b_gat'],m['ln_gamma'],m['ln_beta']])),edges=m['edge_index'])
    nc = _bacc.Bacc("TRN2", target_bir_lowering=False, num_devices=1)
    arrays, args = {}, []
    for name in _NAMES:
        v = _np.ascontiguousarray(ins[name])
        arrays[f"in_{name}_dram"] = v
        args.append(nc.dram_tensor(f"in_{name}_dram", v.shape, _mybir.dt.from_np(v.dtype), kind="ExternalInput").ap())
    args.append(nc.dram_tensor("out_dram", (16384, 64), _mybir.dt.float32, kind="ExternalOutput").ap())
    prog(nc, *args)
    r = _run(nc, [arrays], core_ids=[0])
    return r.results[0]["out_dram"].reshape(64,256,64)
```
